# Optimizing a Trainium2 kernel written in Bass

```python
import numpy as np
import jax
import jax.numpy as jnp

def _softmax(x, axis=-1):
    return jax.nn.softmax(x, axis=axis)

def _gelu(x):
    return jax.nn.gelu(x, approximate=True)

def _silu(x):
    return jax.nn.silu(x)

def _sigmoid(x):
    return jax.nn.sigmoid(x)

def _layernorm(x, axis=-1, eps=1e-05):
    m = jnp.mean(x, axis=axis, keepdims=True)
    v = jnp.var(x, axis=axis, keepdims=True)
    return (x - m) / jnp.sqrt(v + eps)

def _scatter_add(tgt, idx, src, axis=0):
    return tgt.at[idx].add(src)

def _segment_sum(src, seg, n):
    return jax.ops.segment_sum(src, seg, n)
kernel_name = 'mk_metaformer_d1_conv_nhwc128_r4_95fa12'

def setup_inputs(seed: int=0):
    np.random.seed(seed)
    _w = jnp.asarray

    def _rec_inputs():
        import jax
        import jax.numpy as jnp
        _gk = jax.random.key(seed)
        x = -0.000125 + 0.9999 * jax.random.normal(jax.random.fold_in(_gk, 1), (16, 32, 32, 32), jnp.float32)
        return x
    x = _rec_inputs()

    def _L0_conv_setup():
        import jax, jax.numpy as jnp
        import numpy as np
        N, C, H, W = (16, 32, 32, 32)
        key = jax.random.key(seed)
        ks = jax.random.split(key, 11)
        u = lambda k, shape: jax.random.uniform(k, shape, jnp.float32, 0.1, 0.9)
        return {'x': jax.random.normal(ks[0], (N, C, H, W), jnp.float32), 'Wq': jax.random.normal(ks[1], (C, C), jnp.float32) / np.float32(np.sqrt(C)), 'Wk': jax.random.normal(ks[2], (C, C), jnp.float32) / np.float32(np.sqrt(C)), 'Wv': jax.random.normal(ks[3], (C, C), jnp.float32) / np.float32(np.sqrt(C)), 'rq': u(ks[4], (C, H, H)), 'rk': u(ks[5], (C, H, H)), 'rv': u(ks[6], (C, H, H)), 'Gq': u(ks[7], (1,)), 'Gk': u(ks[8], (1,)), 'Gv1': u(ks[9], (1,)), 'Gv2': u(ks[10], (1,))}
    _L0_conv_all = _L0_conv_setup()
    _L0_conv_in = {k: v for k, v in _L0_conv_all.items() if k in ('Wq', 'Wk', 'Wv', 'rq', 'rk', 'rv', 'Gq', 'Gk', 'Gv1', 'Gv2')}
    del _L0_conv_all

    def _L0_ffn_setup():
        import jax, jax.numpy as jnp
        import numpy as np
        BN_EPS = 1e-05
        key = jax.random.key(seed)
        k1, k2, k3 = jax.random.split(key, 3)
        B, T, I, H = (16, 512, 32, 32)
        x = jax.random.normal(k1, (B, T, I), dtype=jnp.float32)
        W = jax.random.normal(k2, (H, I), dtype=jnp.float32) * (1.0 / np.sqrt(I))
        V = jnp.linalg.qr(jax.random.normal(k3, (H, H), dtype=jnp.float32))[0]
        gamma = jnp.ones((H,), dtype=jnp.float32)
        beta = jnp.zeros((H,), dtype=jnp.float32)
        return {'x': x, 'W': W, 'V': V, 'gamma': gamma, 'beta': beta}
    _L0_ffn_all = _L0_ffn_setup()
    _L0_ffn_in = {k: v for k, v in _L0_ffn_all.items() if k in ('W', 'V', 'gamma', 'beta')}
    del _L0_ffn_all
    return {'x': x, 'L0_conv_Wq': _L0_conv_in['Wq'], 'L0_conv_Wk': _L0_conv_in['Wk'], 'L0_conv_Wv': _L0_conv_in['Wv'], 'L0_conv_rq': _L0_conv_in['rq'], 'L0_conv_rk': _L0_conv_in['rk'], 'L0_conv_rv': _L0_conv_in['rv'], 'L0_conv_Gq': _L0_conv_in['Gq'], 'L0_conv_Gk': _L0_conv_in['Gk'], 'L0_conv_Gv1': _L0_conv_in['Gv1'], 'L0_conv_Gv2': _L0_conv_in['Gv2'], 'L0_ffn_W': _L0_ffn_in['W'], 'L0_ffn_V': _L0_ffn_in['V'], 'L0_ffn_gamma': _L0_ffn_in['gamma'], 'L0_ffn_beta': _L0_ffn_in['beta']}

def reference(x, L0_conv_Wq, L0_conv_Wk, L0_conv_Wv, L0_conv_rq, L0_conv_rk, L0_conv_rv, L0_conv_Gq, L0_conv_Gk, L0_conv_Gv1, L0_conv_Gv2, L0_ffn_W, L0_ffn_V, L0_ffn_gamma, L0_ffn_beta):
    import jax
    import jax.numpy as jnp

    def _L0_conv_ref(x, Wq, Wk, Wv, rq, rk, rv, Gq, Gk, Gv1, Gv2):
        import jax, jax.numpy as jnp
        import numpy as np
        N, C, H, W = (16, 32, 32, 32)
        d = np.float32(np.sqrt(C))
        q = jnp.einsum('oc,ncij->noij', Wq, x)
        k = jnp.einsum('oc,ncij->noij', Wk, x)
        v = jnp.einsum('oc,ncij->noij', Wv, x)
        qk = jnp.einsum('ncij,nchj->nihj', q, k) / d
        qrq = jnp.einsum('ncij,chi->nihj', q, rq) / d
        krk = jnp.einsum('ncij,chi->nihj', k, rk) / d
        weight = jax.nn.softmax(qk + Gq * qrq + Gk * krk, axis=3)
        out = jnp.einsum('nihj,nchj->ncij', weight, Gv1 * v) + jnp.einsum('nihj,chi->ncij', weight, Gv2 * rv)
        return out

    def _L0_ffn_ref(x, W, V, gamma, beta):
        import jax, jax.numpy as jnp
        import numpy as np
        BN_EPS = 1e-05
        B, T, H = (x.shape[0], x.shape[1], W.shape[0])
        Wx = jnp.einsum('bti,hi->bth', x, W)
        flat = Wx.reshape(B * T, H)
        mean = jnp.mean(flat, axis=0)
        var = jnp.var(flat, axis=0)
        Wx = ((flat - mean) * jax.lax.rsqrt(var + BN_EPS) * gamma + beta).reshape(B, T, H)
        Vt = V.T

        def step(yt, wx_t):
            yt = jax.nn.sigmoid(wx_t + yt @ Vt)
            return (yt, yt)
        y0 = jnp.zeros((B, H), dtype=Wx.dtype)
        _, ys = jax.lax.scan(step, y0, jnp.swapaxes(Wx, 0, 1))
        return jnp.swapaxes(ys, 0, 1)

    def _gn(v, G=32, eps=1e-05):
        B_, H_, W_, C_ = v.shape
        g = v.reshape(B_, H_, W_, G, C_ // G)
        m = jnp.mean(g, axis=(1, 2, 4), keepdims=True)
        s = jnp.var(g, axis=(1, 2, 4), keepdims=True)
        return ((g - m) / jnp.sqrt(s + eps)).reshape(v.shape)

    def _ln_c(v, eps=1e-06):
        m = jnp.mean(v, axis=-1, keepdims=True)
        s = jnp.var(v, axis=-1, keepdims=True)
        return (v - m) / jnp.sqrt(s + eps)

    def _ln_t(v, eps=1e-05):
        m = jnp.mean(v, axis=-1, keepdims=True)
        s = jnp.var(v, axis=-1, keepdims=True)
        return (v - m) / jnp.sqrt(s + eps)

    def _to_tokens(v):
        B_, H_, W_, C_ = v.shape
        return v.reshape(B_, H_ * W_, C_)

    def _from_tokens(t, like):
        return t.reshape(like.shape)
    x = x + _L0_conv_ref(_ln_c(x), L0_conv_Wq, L0_conv_Wk, L0_conv_Wv, L0_conv_rq, L0_conv_rk, L0_conv_rv, L0_conv_Gq, L0_conv_Gk, L0_conv_Gv1, L0_conv_Gv2)
    t = _to_tokens(x)
    t = t + _L0_ffn_ref(_ln_t(t), L0_ffn_W, L0_ffn_V, L0_ffn_gamma, L0_ffn_beta)
    x = _from_tokens(t, x)
    return x

_drawn_inputs = setup_inputs


def setup_inputs(seed=0):
    import zlib

    import numpy as np

    out = dict(_drawn_inputs(seed))
    spreads = {'L0_ffn_gamma': (1.0, 0.6), 'L0_ffn_beta': (0.0, 0.456)}
    factors = {'L0_conv_rq': 3.801, 'L0_conv_rk': 6.431}
    for name, (base, spread) in spreads.items():
        noise = np.random.default_rng([zlib.crc32(name.encode()), seed]).standard_normal(out[name].shape)
        drawn = base * np.exp(spread * noise) if base else spread * noise
        out[name] = jnp.asarray(drawn.astype(out[name].dtype))
    for name, factor in factors.items():
        out[name] = (out[name] * factor).astype(out[name].dtype)
    return out
```

```python
from contextlib import ExitStack

import concourse.bass as bass
from concourse import mybir

P = 128
G = 4
Q = 4
C = 32
COLS = Q * C * C
IMG = C * C
BANK = 512
ROWS = 4
BLOCKS = C // ROWS
STREAMS = 4
SEG = C // STREAMS
GROUPS = SEG // ROWS
WARM = 12
ROUNDS = WARM + SEG
SEGMENTS = C * STREAMS
AGREE = 2.0 ** -18
LN1_EPS = 1e-6
LN2_EPS = 1e-5
BN_EPS = 1e-5

ALU = mybir.AluOpType
ACT = mybir.ActivationFunctionType
F32 = mybir.dt.float32
I32 = mybir.dt.int32
AX_X = mybir.AxisListType.X


def metaformer_kernel(nc, x, Wq, Wk, Wv, rq, rk, rv, Gq, Gk, Gv1, Gv2, W, V, gamma, beta, out):
    d = float(C) ** 0.5
    x_dram = x.rearrange("(q g) c i j -> q (g c) (i j)", g=G)
    out_dram = out.rearrange("(q g) c i j -> (g c) q (i j)", g=G)

    with ExitStack() as ctx:
        def sb(name, shape, dt=F32):
            return ctx.enter_context(nc.sbuf_tensor(name, shape, dt))

        def sem(name):
            return ctx.enter_context(nc.semaphore(name))

        xin = sb("xin", [P, Q, C, C])
        y = sb("y", [P, Q, C, C])
        u_tile = sb("u_tile", [P, COLS])
        yt_tile = sb("yt_tile", [P, COLS])
        bias_tile = sb("bias_tile", [P, COLS])
        att = sb("att", [P, Q, C, C])
        r_tile = sb("r_tile", [P, COLS])
        rv_bd = sb("rv_bd", [P, C, P])
        x2 = sb("x2", [P, Q, C, C])
        x2n = sb("x2n", [P, Q, C, C])
        u = u_tile[:, :].rearrange("p (q h j) -> p q h j", q=Q, h=C)
        tokens = u_tile[:, :].rearrange("p (i q c) -> p i q c", i=C, q=Q)
        y_t = yt_tile[:, :].rearrange("p (q j c) -> p q j c", q=Q, j=C)
        wx = yt_tile[:, :].rearrange("p (i m) -> p i m", i=C)
        rel = bias_tile[:, :].rearrange("p (q i j) -> p q i j", q=Q, i=C)
        states = bias_tile[:, :].rearrange("p (i q c) -> p i q c", i=C, q=Q)
        r_bd = r_tile[:, :].rearrange("p (i m) -> p i m", i=C)
        wsum = r_tile[:, :].rearrange("p (q i j) -> p q i j", q=Q, i=C)
        result = y

        square = sb("square", [P, 2, IMG])
        stat = sb("stat", [P, 3, Q, C])
        soft = sb("soft", [P, 2, Q, C])
        stat2 = sb("stat2", [P, 3, BLOCKS, Q * ROWS])
        back = sb("back", [P, STREAMS, BANK])
        warm = sb("warm", [P, 2, STREAMS, Q, C + 1])

        wsmall = sb("wsmall", [P, 5, C])
        wturned = sb("wturned", [P, 3, C])
        w_bd = sb("w_bd", [P, 3, P])
        m_bd = sb("m_bd", [P, P])
        r_in = sb("r_in", [C, 3, IMG])
        rv_t = sb("rv_t", [C, C, C])
        spread = sb("spread", [C, 3, P])
        gates = sb("gates", [P, 4])
        affine = sb("affine", [P, 2])
        average = sb("average", [P, G, C])
        ones = sb("ones", [P, 1])
        bn = sb("bn", [P, BLOCKS, 6])
        bnv = sb("bnv", [P, 10])
        diff = square[:, :, :].rearrange("p b (k m) -> p (b k) m", k=2)
        agreed = sb("agreed", [P, 1])
        repeat_flag = sb("repeat_flag", [1, 1], I32)

        ps = ctx.enter_context(nc.psum_tensor("ps", [P, 8, BANK], F32))

        names = """x_in0 x_in1 x_in2 x_in3 w_in r_in_s gates_in affine_in zeros average_set ones_set turned w_spread
        m_product m_set w_set r_product r_set rv_turned rv_product rv_set
        ln_sum ln_mean ln_centred ln_squared ln_sum2 ln_var ln_std ln_rstd y_ready y_turned
        u_product u_half rel_product rel_ready score_product score_sum score_max score_shifted
        score_exp weight_sum weight_recip weights wsum_product wsum_half
        att_product x2_ready t_sum t_mean t_centred t_squared t_sum2 t_var t_std t_rstd t_norm
        t_turned wx_product wx_ready bn_part bn_group bn_zero bn_mean bn_mean_s bn_off bn_spread
        bn_var bn_var_s bn_std bn_rstd bn_scale bn_ms bn_shift
        warm_zero seeded preact state turned_back added stored
        diff_d diff_sq diff_ok agree_sum agree_count flag
        f_marked f_start f_seeded f_preact f_state f_turned f_added""".split()
        S = {n: sem(n) for n in names}
        block = ctx.enter_context(nc.Block())

        def bank(k):
            return ps[:, k, :]

        def half_scores(q, jh):
            return 2 + 2 * (q % 2) + jh

        ATT_BANK = [2, 3, 4, 5]
        WX_BANK = [6, 7, 0, 1]

        def round_row(t):
            return (SEG - WARM % SEG + t) % SEG

        def state_out(t, r):
            if t >= WARM:
                return states[:, SEG * r + round_row(t), :, :]
            return warm[:, (t + SEG - WARM % SEG) // SEG % 2, r, :, 1:C + 1]

        def state_in(t, r):
            if round_row(t) == 0:
                return start_state((t - 1 + SEG - WARM % SEG) // SEG % 2, r)
            return state_out(t - 1, r)

        def start_state(side, r):
            if r == 0:
                return warm[:, side, STREAMS - 1, :, 0:C]
            return warm[:, side, r - 1, :, 1:C + 1]

        FINAL_SIDE = (WARM - 1 + SEG - WARM % SEG) // SEG % 2

        def rec_bank(t, r):
            return 2 * r + round_row(t) // ROWS

        def rec_slot(t, r):
            k = round_row(t) % ROWS
            return ps[:, rec_bank(t, r), P * k:P * (k + 1)]

        @block.sync
        def _(sp):
            for q in range(Q):
                sp.dma_start(xin[:, q, :, :].rearrange("p i j -> p (i j)"), x_dram[q]).then_inc(S[f"x_in{q}"], 16)
            n = 0
            for h in range(GROUPS):
                for r in range(STREAMS):
                    b = GROUPS * r + h
                    n += 1
                    sp.wait_ge(S["added"], n)
                    sp.dma_start(out_dram[:, :, ROWS * C * b:ROWS * C * (b + 1)],
                                 result[:, :, ROWS * b:ROWS * (b + 1), :].rearrange("p q i j -> p q (i j)")
                                 ).then_inc(S["stored"], 16)
            sp.wait_ge(S["stored"], 16 * BLOCKS)
            sp.wait_ge(S["flag"], 1)
            repeat = sp.value_load(repeat_flag[0:1, 0:1], min_val=0, max_val=1)
            with sp.If(repeat == 1):
                sp.wait_ge(S["f_added"], 1)
                sp.dma_start(out_dram, result[:, :, :, :].rearrange("p q i j -> p q (i j)")).then_inc(S["stored"], 16)
                sp.wait_ge(S["stored"], 16 * (BLOCKS + 1))

        @block.gpsimd
        def _(pool):
            nc.gpsimd.memset(w_bd[:, :, :], 0.0)
            nc.gpsimd.memset(m_bd[:, :], 0.0)
            nc.gpsimd.memset(average[:, :, :], 0.0).then_inc(S["zeros"], 1)
            pool.wait_ge(S["zeros"], 1)
            for k in range(1 - G, G):
                ins = nc.gpsimd.affine_select(out=average[:, :, :], in_=average[:, :, :], compare_op=ALU.not_equal,
                                              fill=1.0 / G, base=C * k, pattern=[[-C, G], [-1, C]],
                                              channel_multiplier=1)
                ins.then_inc(S["average_set"], 1)
                pool.wait_ge(S["average_set"], k + G)
            nc.gpsimd.memset(r_tile[:, :], 0.0).then_inc(S["zeros"], 1)
            nc.gpsimd.memset(rv_bd[:, :, :], 0.0).then_inc(S["zeros"], 1)
            nc.gpsimd.memset(ones[:, :], 1.0).then_inc(S["ones_set"], 1)
            nc.gpsimd.memset(warm[:, :, :, :, :], 0.0).then_inc(S["warm_zero"], 1)
            for q in range(Q):
                pool.wait_ge(S["ln_rstd"], q + 1)
                pool.wait_ge(S["ln_squared"], q + 1)
                nc.gpsimd.tensor_tensor(y[:, q, :, :], y[:, q, :, :],
                                        stat[:, 2, q, :].unsqueeze(2).broadcast_to([P, C, C]),
                                        ALU.mult).then_inc(S["y_ready"], 1)
            for q in range(Q):
                pool.wait_ge(S["score_max"], q + 1)
                nc.gpsimd.tensor_tensor(att[:, q, :, :], att[:, q, :, :],
                                        soft[:, 0, q, :].unsqueeze(2).broadcast_to([P, C, C]),
                                        ALU.subtract).then_inc(S["score_shifted"], 1)

            def centre(b):
                rows = slice(ROWS * b, ROWS * (b + 1))
                pool.wait_ge(S["t_mean"], b + 1)
                nc.gpsimd.tensor_tensor(x2n[:, :, rows, :], x2[:, :, rows, :],
                                        stat2[:, 0, b, :].rearrange("p (q i) -> p q i", q=Q).unsqueeze(3)
                                        .broadcast_to([P, Q, ROWS, C]), ALU.subtract).then_inc(S["t_centred"], 1)

            def scale(b):
                rows = slice(ROWS * b, ROWS * (b + 1))
                pool.wait_ge(S["t_rstd"], b + 1)
                pool.wait_ge(S["t_squared"], b + 1)
                nc.gpsimd.tensor_tensor(x2n[:, :, rows, :], x2n[:, :, rows, :],
                                        stat2[:, 2, b, :].rearrange("p (q i) -> p q i", q=Q).unsqueeze(3)
                                        .broadcast_to([P, Q, ROWS, C]), ALU.mult).then_inc(S["t_norm"], 1)

            for t in range(BLOCKS + 2):
                if t < BLOCKS:
                    centre(t)
                if t >= 2:
                    scale(t - 2)

        @block.scalar
        def _(act):
            small = {0: Wv, 1: W, 2: V, 3: Wk, 4: Wq}
            for k in (3, 4, 0, 1, 2):
                act.dma_start(wsmall[:, k, :], bass.AP(small[k].tensor, 0, [[0, G], [C, C], [1, C]])).then_inc(S["w_in"], 16)
            for k, gate in enumerate((Gq, Gk, Gv1, Gv2)):
                act.dma_start(gates[:, k:k + 1], bass.AP(gate.tensor, 0, [[0, P], [1, 1]])).then_inc(S["gates_in"], 16)
            for k, a in enumerate((rq, rk, rv)):
                act.dma_start(r_in[:, k, :], a.rearrange("c h i -> c (h i)")).then_inc(S["r_in_s"], 16)
            for k, a in enumerate((gamma, beta)):
                act.dma_start(affine[:, k:k + 1], bass.AP(a.tensor, 0, [[0, G], [1, C], [1, 1]])).then_inc(S["affine_in"], 16)

            act.wait_ge(S["m_product"], 1)
            act.wait_ge(S["zeros"], 1)
            for g in range(G):
                p = slice(C * g, C * (g + 1))
                nc.scalar.mul(m_bd[p, p], ps[p, 6, 0:C], 1.0 / d).then_inc(S["m_set"], 1)

            def u_half(q, k):
                act.wait_ge(S["u_product"], 2 * q + k + 1)
                nc.scalar.copy(u_tile[:, IMG * q + BANK * k:IMG * q + BANK * (k + 1)], bank(k)).then_inc(S["u_half"], 1)

            for q in range(Q):
                act.wait_ge(S["ln_centred"], q + 1)
                if q >= 2:
                    act.wait_ge(S["ln_sum2"], q - 1)
                nc.scalar.activation(square[:, q % 2, :], y[:, q, :, :].rearrange("p i j -> p (i j)"),
                                     ACT.Square).then_inc(S["ln_squared"], 1)
                act.wait_ge(S["ln_var"], q + 1)
                nc.scalar.activation(stat[:, 2, q, :], stat[:, 1, q, :], ACT.Sqrt).then_inc(S["ln_std"], 1)
                if q == 0:
                    act.wait_ge(S["r_product"], 1)
                    act.wait_ge(S["zeros"], 2)
                    for g in range(G):
                        p = slice(C * g, C * (g + 1))
                        nc.scalar.copy(r_bd[p, :, p], ps[p, 6:8, :].rearrange("p b (h i) -> p i (b h)", i=C)
                                       ).then_inc(S["r_set"], 1)
                if q == 1:
                    u_half(0, 0)
                    u_half(0, 1)
            act.wait_ge(S["rv_product"], 1)
            act.wait_ge(S["zeros"], 3)
            for g in range(G):
                p = slice(C * g, C * (g + 1))
                nc.scalar.copy(rv_bd[p, :, p], ps[p, 6:8, :].rearrange("p b (i c) -> p (b i) c", c=C)
                               ).then_inc(S["rv_set"], 1)
            for q in range(1, Q):
                u_half(q, 0)
                u_half(q, 1)
            for b in range(BLOCKS):
                act.wait_ge(S["rel_product"], b + 1)
                nc.scalar.copy(rel[:, :, ROWS * b:ROWS * (b + 1), :],
                               bank(6 + b % 2).rearrange("p (i q j) -> p q i j", i=ROWS, q=Q)).then_inc(S["rel_ready"], 1)
            for q in range(Q):
                act.wait_ge(S["score_shifted"], q + 1)
                nc.scalar.activation(att[:, q, :, :].rearrange("p i j -> p (i j)"),
                                     att[:, q, :, :].rearrange("p i j -> p (i j)"), ACT.Exp).then_inc(S["score_exp"], 1)
            for q in range(Q):
                for jh in range(2):
                    act.wait_ge(S["wsum_product"], 2 * q + jh + 1)
                    nc.scalar.copy(wsum[:, q, :, 16 * jh:16 * (jh + 1)],
                                   bank(jh).rearrange("p (j i) -> p i j", i=C)).then_inc(S["wsum_half"], 1)

            def t_square(b):
                act.wait_ge(S["t_centred"], b + 1)
                if b >= 2:
                    act.wait_ge(S["t_sum2"], b - 1)
                nc.scalar.activation(square[:, b % 2, 0:BANK].rearrange("p (q i j) -> p q i j", q=Q, i=ROWS),
                                     x2n[:, :, ROWS * b:ROWS * (b + 1), :], ACT.Square).then_inc(S["t_squared"], 1)

            def t_std(b):
                act.wait_ge(S["t_var"], b + 1)
                nc.scalar.activation(stat2[:, 2, b, :], stat2[:, 1, b, :], ACT.Sqrt).then_inc(S["t_std"], 1)

            def wx_out(b):
                act.wait_ge(S["wx_product"], b + 1)
                nc.scalar.copy(yt_tile[:, BANK * b:BANK * (b + 1)], bank(WX_BANK[b % 4])).then_inc(S["wx_ready"], 1)

            for t in range(BLOCKS + 4):
                if t < BLOCKS:
                    t_square(t)
                if 1 <= t <= BLOCKS:
                    t_std(t - 1)
                if t >= 4:
                    wx_out(t - 4)
            act.wait_ge(S["bn_var_s"], 1)
            nc.scalar.activation(bnv[:, 6:7], bnv[:, 5:6], ACT.Sqrt).then_inc(S["bn_std"], 1)

            for t in range(ROUNDS):
                for r in range(STREAMS):
                    if t == 0:
                        act.wait_ge(S["seeded"], r + 1)
                        act.wait_ge(S["warm_zero"], 1)
                    else:
                        act.wait_ge(S["preact"], STREAMS * (t - 1) + r + 1)
                    nc.scalar.activation(state_out(t, r), rec_slot(t, r).rearrange("p (q c) -> p q c", q=Q),
                                         ACT.Sigmoid).then_inc(S["state"], 1)

            act.wait_ge(S["flag"], 1)
            repeat = act.value_load(repeat_flag[0:1, 0:1], min_val=0, max_val=1)
            with act.If(repeat == 1):
                with act.Fori(0, SEGMENTS - 1) as n:
                    for s in range(SEG):
                        for r in range(STREAMS):
                            act.wait_ge(S["f_preact"], n * (SEG * STREAMS) + (STREAMS * s + r + 1))
                            nc.scalar.activation(states[:, SEG * r + s, :, :],
                                                 rec_slot(WARM + s, r).rearrange("p (q c) -> p q c", q=Q),
                                                 ACT.Sigmoid).then_inc(S["f_state"], 1)

        @block.vector
        def _(dve):
            dve.wait_ge(S["w_in"], 16 * 5)
            dve.wait_ge(S["gates_in"], 16 * 4)
            nc.vector.transpose(wturned[:, :, :], wsmall[:, 0:3, :]).then_inc(S["turned"], 1)
            dve.wait_ge(S["average_set"], 2 * G - 1)
            for k, (src, gate, factor) in enumerate(((wsmall[0:C, 4, :], gates[0:C, 0:1], 1.0 / d),
                                                     (wsmall[0:C, 3, :], gates[0:C, 1:2], 1.0 / d),
                                                     (average[0:C, 0, :], gates[0:C, 3:4], float(G)))):
                nc.vector.tensor_scalar(spread[:, k, :].rearrange("p (g c) -> p g c", g=G),
                                        src.unsqueeze(1).broadcast_to([C, G, C]), gate, factor,
                                        ALU.mult, ALU.mult).then_inc(S["w_spread"], 1)
            dve.wait_ge(S["turned"], 1)
            dve.wait_ge(S["zeros"], 1)
            for g in range(G):
                p = slice(C * g, C * (g + 1))
                nc.vector.tensor_scalar(w_bd[p, 0, p], wturned[p, 0, :], gates[p, 2:3], None,
                                        ALU.mult).then_inc(S["w_set"], 1)
                nc.vector.tensor_copy(w_bd[p, 1:3, p], wturned[p, 1:3, :]).then_inc(S["w_set"], 1)
            dve.wait_ge(S["r_in_s"], 16 * 3)
            nc.vector.transpose(rv_t[:, :, :], r_in[:, 2, :].rearrange("p (h i) -> p i h", h=C)).then_inc(S["rv_turned"], 1)

            def ln_centre(q):
                dve.wait_ge(S[f"x_in{q}"], 16)
                nc.vector.tensor_reduce(stat[:, 1, q, :], xin[:, q, :, :], AX_X, ALU.add).then_inc(S["ln_sum"], 1)
                dve.wait_ge(S["ln_sum"], q + 1)
                nc.vector.tensor_scalar(stat[:, 0, q, :], stat[:, 1, q, :], 1.0 / C, None, ALU.mult).then_inc(S["ln_mean"], 1)
                dve.wait_ge(S["ln_mean"], q + 1)
                nc.vector.tensor_tensor(y[:, q, :, :], xin[:, q, :, :],
                                        stat[:, 0, q, :].unsqueeze(2).broadcast_to([P, C, C]),
                                        ALU.subtract).then_inc(S["ln_centred"], 1)

            def ln_var(q):
                dve.wait_ge(S["ln_squared"], q + 1)
                nc.vector.tensor_reduce(stat[:, 0, q, :], square[:, q % 2, :].rearrange("p (i j) -> p i j", i=C),
                                        AX_X, ALU.add).then_inc(S["ln_sum2"], 1)
                dve.wait_ge(S["ln_sum2"], q + 1)
                nc.vector.tensor_scalar(stat[:, 1, q, :], stat[:, 0, q, :], 1.0 / C, LN1_EPS,
                                        ALU.mult, ALU.add).then_inc(S["ln_var"], 1)

            def ln_rstd(q):
                dve.wait_ge(S["ln_std"], q + 1)
                nc.vector.reciprocal(stat[:, 2, q, :], stat[:, 2, q, :]).then_inc(S["ln_rstd"], 1)

            for t in range(Q + 1):
                if t < Q:
                    ln_centre(t)
                if t >= 1:
                    ln_var(t - 1)
                    ln_rstd(t - 1)
            for q in range(Q):
                dve.wait_ge(S["y_ready"], q + 1)
                nc.vector.transpose(y_t[:, q, :, :], y[:, q, :, :].rearrange("p h j -> p j h")).then_inc(S["y_turned"], 1)

            def score_max(q):
                dve.wait_ge(S["score_product"], 2 * q + 2)
                dve.wait_ge(S["rel_ready"], BLOCKS)
                nc.vector.tensor_tensor(att[:, q, :, :],
                                        ps[:, half_scores(q, 0):half_scores(q, 0) + 2, :]
                                        .rearrange("p b (j i) -> p i (b j)", i=C),
                                        rel[:, q, :, :], ALU.add).then_inc(S["score_sum"], 1)
                dve.wait_ge(S["score_sum"], q + 1)
                nc.vector.tensor_reduce(soft[:, 0, q, :], att[:, q, :, :], AX_X, ALU.max).then_inc(S["score_max"], 1)

            def weights(q):
                dve.wait_ge(S["score_exp"], q + 1)
                nc.vector.tensor_reduce(soft[:, 1, q, :], att[:, q, :, :], AX_X, ALU.add).then_inc(S["weight_sum"], 1)
                dve.wait_ge(S["weight_sum"], q + 1)
                nc.vector.reciprocal(soft[:, 1, q, :], soft[:, 1, q, :]).then_inc(S["weight_recip"], 1)
                dve.wait_ge(S["weight_recip"], q + 1)
                nc.vector.tensor_tensor(att[:, q, :, :], att[:, q, :, :],
                                        soft[:, 1, q, :].unsqueeze(2).broadcast_to([P, C, C]),
                                        ALU.mult).then_inc(S["weights"], 1)

            for t in range(Q + 1):
                if t < Q:
                    score_max(t)
                if t >= 1:
                    weights(t - 1)

            def residual(b):
                rows = slice(ROWS * b, ROWS * (b + 1))
                dve.wait_ge(S["att_product"], b + 1)
                nc.vector.tensor_tensor(x2[:, :, rows, :],
                                        bank(ATT_BANK[b % 4]).rearrange("p (q i j) -> p q i j", q=Q, i=ROWS),
                                        xin[:, :, rows, :], ALU.add).then_inc(S["x2_ready"], 1)
                dve.wait_ge(S["x2_ready"], b + 1)
                nc.vector.tensor_reduce(stat2[:, 1, b, :].rearrange("p (q i) -> p q i", q=Q), x2[:, :, rows, :],
                                        AX_X, ALU.add).then_inc(S["t_sum"], 1)
                dve.wait_ge(S["t_sum"], b + 1)
                nc.vector.tensor_scalar(stat2[:, 0, b, :], stat2[:, 1, b, :], 1.0 / C, None, ALU.mult).then_inc(S["t_mean"], 1)

            def t_var(b):
                dve.wait_ge(S["t_squared"], b + 1)
                nc.vector.tensor_reduce(stat2[:, 0, b, :], square[:, b % 2, 0:BANK].rearrange("p (m j) -> p m j", j=C),
                                        AX_X, ALU.add).then_inc(S["t_sum2"], 1)
                dve.wait_ge(S["t_sum2"], b + 1)
                nc.vector.tensor_scalar(stat2[:, 1, b, :], stat2[:, 0, b, :], 1.0 / C, LN2_EPS,
                                        ALU.mult, ALU.add).then_inc(S["t_var"], 1)

            def t_rstd(b):
                dve.wait_ge(S["t_std"], b + 1)
                nc.vector.reciprocal(stat2[:, 2, b, :], stat2[:, 2, b, :]).then_inc(S["t_rstd"], 1)

            def t_turn(b):
                rows = slice(ROWS * b, ROWS * (b + 1))
                dve.wait_ge(S["t_norm"], b + 1)
                nc.vector.transpose(tokens[:, rows, :, :],
                                    x2n[:, :, rows, :].rearrange("p q i j -> p i q j")).then_inc(S["t_turned"], 1)

            def bn_part(b):
                dve.wait_ge(S["wx_ready"], b + 1)
                nc.vector.bn_stats(bn[:, b, :], yt_tile[:, BANK * b:BANK * (b + 1)]).then_inc(S["bn_part"], 1)

            for t in range(BLOCKS + 5):
                if t < BLOCKS:
                    residual(t)
                if 1 <= t <= BLOCKS:
                    t_var(t - 1)
                if 2 <= t <= BLOCKS + 1:
                    t_rstd(t - 2)
                if 3 <= t <= BLOCKS + 2:
                    t_turn(t - 3)
                if t >= 5:
                    bn_part(t - 5)

            gmean, gvar, mean, off, spr, var, std, scl, ms, shift = (bnv[:, k:k + 1] for k in range(10))
            nc.vector.memset(ps[:, 7, 0:2], 0.0).then_inc(S["bn_zero"], 1)
            dve.wait_ge(S["bn_part"], BLOCKS)
            nc.vector.bn_aggr(bnv[:, 0:2], bn[:, :, :]).then_inc(S["bn_group"], 1)
            dve.wait_ge(S["bn_mean"], 1)
            nc.vector.tensor_copy(mean, ps[:, 7, 0:1]).then_inc(S["bn_mean_s"], 1)
            dve.wait_ge(S["bn_mean_s"], 1)
            nc.vector.tensor_tensor(off, gmean, mean, ALU.subtract).then_inc(S["bn_off"], 1)
            dve.wait_ge(S["bn_off"], 1)
            nc.vector.scalar_tensor_tensor(out=spr, in0=off, scalar=off, in1=gvar, op0=ALU.mult,
                                           op1=ALU.add).then_inc(S["bn_spread"], 1)
            dve.wait_ge(S["bn_var"], 1)
            nc.vector.tensor_scalar(var, ps[:, 7, 1:2], BN_EPS, None, ALU.add).then_inc(S["bn_var_s"], 1)
            dve.wait_ge(S["bn_std"], 1)
            dve.wait_ge(S["affine_in"], 32)
            nc.vector.reciprocal(std, std).then_inc(S["bn_rstd"], 1)
            dve.wait_ge(S["bn_rstd"], 1)
            nc.vector.tensor_tensor(scl, std, affine[:, 0:1], ALU.mult).then_inc(S["bn_scale"], 1)
            dve.wait_ge(S["bn_scale"], 1)
            nc.vector.tensor_tensor(ms, mean, scl, ALU.mult).then_inc(S["bn_ms"], 1)
            dve.wait_ge(S["bn_ms"], 1)
            nc.vector.tensor_tensor(shift, affine[:, 1:2], ms, ALU.subtract).then_inc(S["bn_shift"], 1)
            dve.wait_ge(S["bn_shift"], 1)

            def seed(t, r):
                row = SEG * r + round_row(t)
                return nc.vector.tensor_scalar(bank(rec_bank(t, r)), wx[:, row:row + ROWS, :].rearrange("p i m -> p (i m)"),
                                               scl, shift, ALU.mult, ALU.add)

            def turn_back(h, r, done):
                b = GROUPS * r + h
                nc.vector.transpose(back[:, r, :].rearrange("p (q i j) -> p i q j", q=Q, i=ROWS),
                                    states[:, ROWS * b:ROWS * (b + 1), :, :]).then_inc(done, 1)

            def add_back(h, r, done):
                rows = slice(ROWS * (GROUPS * r + h), ROWS * (GROUPS * r + h + 1))
                nc.vector.tensor_tensor(result[:, :, rows, :], back[:, r, :].rearrange("p (q i j) -> p q i j", q=Q, i=ROWS),
                                        x2[:, :, rows, :], ALU.add).then_inc(done, 1)

            nturn = 0
            for n in range(ROUNDS // ROWS + 1):
                if n < ROUNDS // ROWS:
                    for r in range(STREAMS):
                        if n >= 2:
                            dve.wait_ge(S["state"], STREAMS * (ROWS * (n - 1) - 1) + r + 1)
                        seed(ROWS * n, r).then_inc(S["seeded"], 1)
                h = n - 1 - WARM // ROWS
                if h >= 0:
                    for r in range(STREAMS):
                        dve.wait_ge(S["state"], STREAMS * (ROWS * n - 1) + r + 1)
                        if nturn >= STREAMS:
                            dve.wait_ge(S["added"], nturn - STREAMS + 1)
                        nturn += 1
                        turn_back(h, r, S["turned_back"])
                        dve.wait_ge(S["turned_back"], nturn)
                        add_back(h, r, S["added"])

            dve.wait_ge(S["state"], STREAMS * ROUNDS)
            nc.vector.tensor_tensor(diff[:, 0, :].rearrange("p (r q c) -> p r q c", r=STREAMS, q=Q),
                                    states[:, SEG - 1::SEG, :, :], warm[:, FINAL_SIDE, :, :, 1:C + 1],
                                    ALU.subtract).then_inc(S["diff_d"], 1)
            dve.wait_ge(S["diff_d"], 1)
            nc.vector.tensor_tensor(diff[:, 1, :], diff[:, 0, :], diff[:, 0, :], ALU.mult).then_inc(S["diff_sq"], 1)
            dve.wait_ge(S["diff_sq"], 1)
            nc.vector.tensor_scalar(diff[:, 2, :], diff[:, 1, :], AGREE * AGREE, None, ALU.is_le).then_inc(S["diff_ok"], 1)
            dve.wait_ge(S["diff_ok"], 1)
            nc.vector.tensor_reduce(agreed[:, :], diff[:, 2, :], AX_X, ALU.add).then_inc(S["agree_sum"], 1)
            dve.wait_ge(S["agree_count"], 1)
            nc.vector.tensor_scalar(repeat_flag[:, :], ps[0:1, 0, 0:1], float(P * STREAMS * Q * C), None,
                                    ALU.is_lt).then_inc(S["flag"], 1)
            dve.wait_ge(S["flag"], 1)
            repeat = dve.value_load(repeat_flag[0:1, 0:1], min_val=0, max_val=1)
            with dve.If(repeat == 1):
                PASS = SEG * STREAMS
                dve.wait_ge(S["f_marked"], 1)
                with dve.Fori(0, SEGMENTS - 1) as n:
                    nc.vector.tensor_copy(warm[:, FINAL_SIDE, :, :, 1:C + 1], states[:, SEG - 1::SEG, :, :]).then_inc(S["f_start"], 1)
                    for h in range(GROUPS):
                        for r in range(STREAMS):
                            seed(WARM + ROWS * h, r).then_inc(S["f_seeded"], 1)
                    dve.wait_ge(S["f_state"], n * PASS + PASS)
                dve.wait_ge(S["stored"], 16 * BLOCKS)
                nturn = 0
                for h in range(GROUPS):
                    for r in range(STREAMS):
                        nturn += 1
                        turn_back(h, r, S["f_turned"])
                        dve.wait_ge(S["f_turned"], nturn)
                        add_back(h, r, S["f_turned"])
                        nturn += 1
                        dve.wait_ge(S["f_turned"], nturn)
                nc.vector.tensor_copy(agreed[:, :], diff[:, 0, 0:1]).then_inc(S["f_added"], 1)

        @block.tensor
        def _(pe):
            pe.wait_ge(S["w_in"], 16 * 5)
            for g in range(G):
                p = slice(C * g, C * (g + 1))
                ins = nc.tensor.matmul(ps[p, 6, 0:C], wsmall[p, 3, :], wsmall[p, 4, :], start=True, stop=True)
            ins.then_inc(S["m_product"], 1)
            pe.wait_ge(S["w_spread"], 3)
            pe.wait_ge(S["r_in_s"], 16 * 3)
            pe.wait_ge(S["m_set"], G)
            for k in range(2):
                cols = slice(BANK * k, BANK * (k + 1))
                nc.tensor.matmul(bank(6 + k), spread[:, 0, :], r_in[:, 0, cols], start=True, stop=False)
                ins = nc.tensor.matmul(bank(6 + k), spread[:, 1, :], r_in[:, 1, cols], start=False, stop=True)
            ins.then_inc(S["r_product"], 1)

            def project_u(q):
                for k in range(2):
                    if q >= 1:
                        pe.wait_ge(S["u_half"], 2 * (q - 1) + k + 1)
                    nc.tensor.matmul(bank(k), m_bd[:, :], y[:, q, 16 * k:16 * (k + 1), :].rearrange("p i j -> p (i j)"),
                                     start=True, stop=True).then_inc(S["u_product"], 1)

            def scores(q):
                pe.wait_ge(S["u_half"], 2 * q + 2)
                if q >= 2:
                    pe.wait_ge(S["score_sum"], q - 1)
                for j in range(C):
                    for g in range(G):
                        p = slice(C * g, C * (g + 1))
                        ins = nc.tensor.matmul(ps[p, half_scores(q, j // 16), C * (j % 16):C * (j % 16 + 1)],
                                               u[p, q, :, j], y[p, q, :, j], start=True, stop=True)
                    if j % 16 == 15:
                        ins.then_inc(S["score_product"], 1)

            for q in range(Q):
                pe.wait_ge(S["y_ready"], q + 1)
                project_u(q)
                if q == 0:
                    pe.wait_ge(S["r_set"], G)
                    pe.wait_ge(S["rv_turned"], 1)
                    for k in range(2):
                        ins = nc.tensor.matmul(bank(6 + k), spread[:, 2, :],
                                               rv_t[:, 16 * k:16 * (k + 1), :].rearrange("p i c -> p (i c)"),
                                               start=True, stop=True)
                    ins.then_inc(S["rv_product"], 1)
                    scores(0)
            scores(1)
            pe.wait_ge(S["rv_set"], G)
            for b in range(BLOCKS):
                if b >= 2:
                    pe.wait_ge(S["rel_ready"], b - 1)
                for k in range(ROWS):
                    ins = nc.tensor.matmul(bank(6 + b % 2)[:, P * k:P * (k + 1)], r_bd[:, ROWS * b + k, :],
                                           y[:, :, ROWS * b + k, :], start=True, stop=True)
                ins.then_inc(S["rel_product"], 1)
            scores(2)
            scores(3)

            for q in range(Q):
                pe.wait_ge(S["weights"], q + 1)
                pe.wait_ge(S["y_turned"], q + 1)
                for j in range(C):
                    if j % 16 == 0 and q >= 1:
                        pe.wait_ge(S["wsum_half"], 2 * (q - 1) + j // 16 + 1)
                    for g in range(G):
                        p = slice(C * g, C * (g + 1))
                        ins = nc.tensor.matmul(ps[p, j // 16, C * (j % 16):C * (j % 16 + 1)],
                                               y_t[p, q, j, :], att[p, q, :, j], start=True, stop=True)
                    if j % 16 == 15:
                        ins.then_inc(S["wsum_product"], 1)

            pe.wait_ge(S["wsum_half"], 2 * Q)
            pe.wait_ge(S["w_set"], 2 * G)

            def attention_out(b):
                if b < 4:
                    pe.wait_ge(S["score_sum"], Q)
                else:
                    pe.wait_ge(S["x2_ready"], b - 3)
                rows = bank(ATT_BANK[b % 4]).rearrange("p (q i j) -> p q i j", q=Q, i=ROWS)
                nc.tensor.matmul(rows, w_bd[:, 0, :], wsum[:, :, ROWS * b:ROWS * (b + 1), :], start=True, stop=True)
                for k in range(ROWS):
                    ins = nc.tensor.matmul(rows[:, :, k, :], rv_bd[:, ROWS * b + k, :], att[:, :, ROWS * b + k, :],
                                           start=False, stop=True, skip_group_check=True)
                ins.then_inc(S["att_product"], 1)

            def project_wx(b):
                pe.wait_ge(S["t_turned"], b + 1)
                if b >= 4:
                    pe.wait_ge(S["wx_ready"], b - 3)
                nc.tensor.matmul(bank(WX_BANK[b % 4]), w_bd[:, 1, :], u_tile[:, BANK * b:BANK * (b + 1)],
                                 start=True, stop=True).then_inc(S["wx_product"], 1)

            for t in range(BLOCKS + 4):
                if t < BLOCKS:
                    attention_out(t)
                if t >= 4:
                    project_wx(t - 4)

            pe.wait_ge(S["bn_zero"], 1)
            pe.wait_ge(S["bn_group"], 1)
            avg = average[:, :, :].rearrange("p g c -> p (g c)")
            nc.tensor.matmul(ps[:, 7, 0:1], avg, bnv[:, 0:1], start=False, stop=True,
                             skip_group_check=True).then_inc(S["bn_mean"], 1)
            pe.wait_ge(S["bn_spread"], 1)
            nc.tensor.matmul(ps[:, 7, 1:2], avg, bnv[:, 4:5], start=False, stop=True,
                             skip_group_check=True).then_inc(S["bn_var"], 1)

            for t in range(1, ROUNDS):
                for r in range(STREAMS):
                    if t % ROWS == 0:
                        pe.wait_ge(S["seeded"], STREAMS * (t // ROWS) + r + 1)
                    src = (r - 1) % STREAMS if round_row(t) == 0 else r
                    pe.wait_ge(S["state"], STREAMS * (t - 1) + src + 1)
                    nc.tensor.matmul(rec_slot(t, r), w_bd[:, 2, :], state_in(t, r), start=False, stop=True,
                                     skip_group_check=True).then_inc(S["preact"], 1)

            pe.wait_ge(S["agree_sum"], 1)
            nc.tensor.matmul(ps[0:1, 0, 0:1], agreed[:, :], ones[:, :], start=True, stop=True).then_inc(S["agree_count"], 1)
            pe.wait_ge(S["flag"], 1)
            repeat = pe.value_load(repeat_flag[0:1, 0:1], min_val=0, max_val=1)
            with pe.If(repeat == 1):
                nc.tensor.matmul(bank(0), w_bd[:, 2, :], wx[:, 0:ROWS, :].rearrange("p i m -> p (i m)"),
                                 start=True, stop=True).then_inc(S["f_marked"], 1)
                with pe.Fori(0, SEGMENTS - 1) as n:
                    pe.wait_ge(S["f_start"], n + 1)
                    for s in range(SEG):
                        for r in range(STREAMS):
                            if s % ROWS == 0:
                                pe.wait_ge(S["f_seeded"], n * (GROUPS * STREAMS) + (STREAMS * (s // ROWS) + r + 1))
                            if s > 0:
                                pe.wait_ge(S["f_state"], n * (SEG * STREAMS) + (STREAMS * (s - 1) + r + 1))
                            nc.tensor.matmul(rec_slot(WARM + s, r), w_bd[:, 2, :],
                                             start_state(FINAL_SIDE, r) if s == 0 else states[:, SEG * r + s - 1, :, :],
                                             start=False, stop=True, skip_group_check=True).then_inc(S["f_preact"], 1)


_INS = ["x", "L0_conv_Wq", "L0_conv_Wk", "L0_conv_Wv", "L0_conv_rq", "L0_conv_rk", "L0_conv_rv", "L0_conv_Gq",
        "L0_conv_Gk", "L0_conv_Gv1", "L0_conv_Gv2", "L0_ffn_W", "L0_ffn_V", "L0_ffn_gamma", "L0_ffn_beta"]
_OUTS = [((16, 32, 32, 32), "float32")]


def kernel(**inputs):
    import numpy as _np
    import concourse.bacc as _bacc
    from concourse import mybir as _mybir
    from concourse.bass_utils import run_bass_kernel_spmd as _run

    nc = _bacc.Bacc("TRN2", target_bir_lowering=False, num_devices=1)
    arrays, args = {}, []
    for name in _INS:
        a = _np.ascontiguousarray(inputs[name])
        arrays[f"in_{name}_dram"] = a
        args.append(nc.dram_tensor(f"in_{name}_dram", a.shape, _mybir.dt.from_np(a.dtype), kind="ExternalInput").ap())
    for i, (shape, dtype) in enumerate(_OUTS):
        dt = _mybir.dt.from_np(_np.dtype(dtype))
        args.append(nc.dram_tensor(f"out_{i}_dram", shape, dt, kind="ExternalOutput").ap())
    metaformer_kernel(nc, *args)
    r = _run(nc, [arrays], core_ids=[0])
    got = tuple(r.results[0][f"out_{i}_dram"] for i in range(len(_OUTS)))
    return got[0]
```

```python
from contextlib import ExitStack

import concourse.bass as bass
from concourse import mybir

P = 128
G = 4
Q = 4
C = 32
COLS = Q * C * C
IMG = C * C
BANK = 512
ROWS = 4
BLOCKS = C // ROWS
STREAMS = 4
SEG = C // STREAMS
GROUPS = SEG // ROWS
UNITS = 2 * Q
WARM = 10
ROUNDS = WARM + SEG
SEGMENTS = C * STREAMS
PIECES = [(0, 2), (2, 2), (4, 2), (6, 2)]
AGREE = 2.0 ** -18
LN1_EPS = 1e-6
LN2_EPS = 1e-5
BN_EPS = 1e-5

ALU = mybir.AluOpType
ACT = mybir.ActivationFunctionType
F32 = mybir.dt.float32
I32 = mybir.dt.int32
AX_X = mybir.AxisListType.X


def metaformer_kernel(nc, x, Wq, Wk, Wv, rq, rk, rv, Gq, Gk, Gv1, Gv2, W, V, gamma, beta, out):
    d = float(C) ** 0.5
    x_dram = x.rearrange("(q g) c i j -> q (g c) (i j)", g=G)
    out_dram = out.rearrange("(q g) c i j -> (g c) q (i j)", g=G)

    with ExitStack() as ctx:
        def sb(name, shape, dt=F32):
            return ctx.enter_context(nc.sbuf_tensor(name, shape, dt))

        def sem(name):
            return ctx.enter_context(nc.semaphore(name))

        xin = sb("xin", [P, Q, C, C])
        y = sb("y", [P, Q, C, C])
        u_tile = sb("u_tile", [P, COLS])
        yt_tile = sb("yt_tile", [P, COLS])
        bias_tile = sb("bias_tile", [P, COLS])
        att = sb("att", [P, Q, C, C])
        r_tile = sb("r_tile", [P, COLS])
        rv_bd = sb("rv_bd", [P, C, P])
        x2 = sb("x2", [P, Q, C, C])
        x2n = sb("x2n", [P, Q, C, C])
        wx_q = bias_tile[:, :].rearrange("p (i q c) -> p i q c", i=C, q=Q)
        u = u_tile[:, :].rearrange("p (q h j) -> p q h j", q=Q, h=C)
        tokens = u_tile[:, :].rearrange("p (i q c) -> p i q c", i=C, q=Q)
        y_t = yt_tile[:, :].rearrange("p (q j c) -> p q j c", q=Q, j=C)
        wx = bias_tile[:, :].rearrange("p (i m) -> p i m", i=C)
        rel = bias_tile[:, :].rearrange("p (q i j) -> p q i j", q=Q, i=C)
        states = yt_tile[:, :].rearrange("p (i q c) -> p i q c", i=C, q=Q)
        r_bd = r_tile[:, :].rearrange("p (i m) -> p i m", i=C)
        wsum = r_tile[:, :].rearrange("p (q i j) -> p q i j", q=Q, i=C)
        result = y

        square = sb("square", [P, 2, IMG])
        stat = sb("stat", [P, 3, Q, C])
        soft = sb("soft", [P, 2, Q, C])
        stat2 = sb("stat2", [P, 3, UNITS, C // 2])
        back = sb("back", [P, STREAMS, BANK])
        warm = sb("warm", [P, 2, STREAMS, Q, C + 1])

        wsmall = sb("wsmall", [P, 5, C])
        wturned = sb("wturned", [P, 3, C])
        w_bd = sb("w_bd", [P, 3, P])
        m_bd = sb("m_bd", [P, P])
        r_in = sb("r_in", [C, 3, IMG])
        rv_t = sb("rv_t", [C, C, C])
        spread = sb("spread", [C, 3, P])
        gates = sb("gates", [P, 4])
        affine = sb("affine", [P, 2])
        average = sb("average", [P, G, C])
        ones = sb("ones", [P, 1])
        bn = sb("bn", [P, BLOCKS, 6])
        bnv = sb("bnv", [P, 10])
        diff = square[:, :, :].rearrange("p b (k m) -> p (b k) m", k=2)
        agreed = sb("agreed", [P, 1])
        diffsum = sb("diffsum", [P, 1])
        repeat_flag = sb("repeat_flag", [1, 1], I32)

        ps = ctx.enter_context(nc.psum_tensor("ps", [P, 8, BANK], F32))

        names = """x_in0 x_in1 x_in2 x_in3 wqk_in w_in r_in_s rv_in gates_in gates2_in affine_in zeros average_set ones_set turned w_spread
        m_product m_set w_set r_product r_set rv_turned rv_product rv_set
        ln_sum ln_mean ln_centred ln_squared ln_sum2 ln_var ln_std ln_rstd y0_ready y_ready y_turned
        u_product u_half rel_product rel_ready score_product score_sum score_max score_shifted
        score_exp weight_sum weight_recip weights wsum_product wsum_half
        relv_product x2_part proj_product t_centred_dve x2_ready t_sum t_mean t_centred t_squared t_sum2 t_var t_std t_rstd t_norm
        t_turned wx_product wx_ready bn_part bn_group bn_zero bn_mean bn_mean_s bn_off bn_spread
        bn_var bn_var_s bn_std bn_rstd bn_scale bn_ms bn_shift
        warm_zero seeded preact state turned_back added_dve added_pool stored
        diff_d diff_sum agreed agree_count flag
        f_marked f_start f_seeded f_preact f_state f_turned""".split()
        S = {n: sem(n) for n in names}
        block = ctx.enter_context(nc.Block())

        def bank(k):
            return ps[:, k, :]

        def half_scores(q, jh):
            return 2 + 2 * (q % 2) + jh

        def wait_y(eng, q):
            if q == 0:
                eng.wait_ge(S["y0_ready"], 1)
            else:
                eng.wait_ge(S["y_ready"], q)

        ATT_BANK = [2, 3, 4, 5]
        PROJ_BANK = [6, 7, 6, 7, 6, 7, 0, 1]
        WX_BANK = [2, 3]

        def unit(t, k):
            return t[:, k // 2, 16 * (k % 2):16 * (k % 2 + 1), :]

        def wx_rows(k):
            return wx_q[:, 16 * (k % 2):16 * (k % 2 + 1), k // 2, :]

        def round_row(t):
            return (t - WARM) % SEG

        def side(t):
            return ((t - WARM) // SEG) % 2

        def state_out(t, r):
            if t >= WARM:
                return states[:, SEG * r + round_row(t), :, :]
            return warm[:, side(t), r, :, 1:C + 1]

        def state_in(t, r):
            if round_row(t) == 0:
                return start_state(side(t - 1), r)
            return state_out(t - 1, r)

        def start_state(k, r):
            if r == 0:
                return warm[:, k, STREAMS - 1, :, 0:C]
            return warm[:, k, r - 1, :, 1:C + 1]

        STORED = 16 * len(PIECES) * STREAMS
        FINAL_SIDE = side(WARM - 1)
        SEEDS = []
        for t in range(ROUNDS):
            if t == 0 or round_row(t) % ROWS == 0:
                SEEDS.append([t, 0])
            SEEDS[-1][1] += 1
        SEED_OF = [n for n, (t, k) in enumerate(SEEDS) for _ in range(k)]

        def rec_bank(t, r):
            return 2 * r + round_row(t) // ROWS

        def rec_slot(t, r):
            k = round_row(t) % ROWS
            return ps[:, rec_bank(t, r), P * k:P * (k + 1)]

        @block.sync
        def _(sp):
            def load_x(q):
                sp.dma_start(xin[:, q, :, :].rearrange("p i j -> p (i j)"), x_dram[q]).then_inc(S[f"x_in{q}"], 16)

            def load_small(k, w, done):
                sp.dma_start(wsmall[:, k, :], bass.AP(w.tensor, 0, [[0, G], [C, C], [1, C]])).then_inc(S[done], 16)

            def load_gate(k, gate, done):
                sp.dma_start(gates[:, k:k + 1], bass.AP(gate.tensor, 0, [[0, P], [1, 1]])).then_inc(S[done], 16)

            def load_rel(k, a, done):
                sp.dma_start(r_in[:, k, :], a.rearrange("c h i -> c (h i)")).then_inc(S[done], 16)

            load_x(0)
            load_small(3, Wk, "wqk_in")
            load_small(4, Wq, "wqk_in")
            load_gate(0, Gq, "gates_in")
            load_gate(1, Gk, "gates_in")
            load_x(1)
            load_rel(0, rq, "r_in_s")
            load_rel(1, rk, "r_in_s")
            load_x(2)
            load_x(3)
            load_rel(2, rv, "rv_in")
            load_small(0, Wv, "w_in")
            load_small(1, W, "w_in")
            load_small(2, V, "w_in")
            load_gate(2, Gv1, "gates2_in")
            load_gate(3, Gv2, "gates2_in")
            for k, a in enumerate((gamma, beta)):
                sp.dma_start(affine[:, k:k + 1], bass.AP(a.tensor, 0, [[0, G], [1, C], [1, 1]])).then_inc(S["affine_in"], 16)
            for n, (row, k) in enumerate(PIECES):
                for r in range(STREAMS):
                    done = S["added_dve"] if r % 2 else S["added_pool"]
                    sp.wait_ge(done, 2 * n + r // 2 + 1)
                    rows = slice(SEG * r + row, SEG * r + row + k)
                    sp.dma_start(out_dram[:, :, C * rows.start:C * rows.stop],
                                 result[:, :, rows, :].rearrange("p q i j -> p q (i j)")).then_inc(S["stored"], 16)
            sp.wait_ge(S["stored"], STORED)
            sp.wait_ge(S["flag"], 1)
            repeat = sp.value_load(repeat_flag[0:1, 0:1], min_val=0, max_val=1)
            with sp.If(repeat == 1):
                sp.wait_ge(S["f_turned"], 2 * BLOCKS)
                sp.dma_start(out_dram, result[:, :, :, :].rearrange("p q i j -> p q (i j)")).then_inc(S["stored"], 16)
                sp.wait_ge(S["stored"], STORED + 16)

        def turn_back(row, k, r):
            rows = slice(SEG * r + row, SEG * r + row + k)
            return nc.vector.transpose(back[:, r, 0:P * k].rearrange("p (q i j) -> p i q j", q=Q, i=k),
                                       states[:, rows, :, :])

        def add_back(eng, row, k, r):
            rows = slice(SEG * r + row, SEG * r + row + k)
            return eng.tensor_tensor(result[:, :, rows, :], back[:, r, 0:P * k].rearrange("p (q i j) -> p q i j", q=Q, i=k),
                                     x2[:, :, rows, :], ALU.add)

        @block.gpsimd
        def _(pool):
            nc.gpsimd.memset(w_bd[:, :, :], 0.0)
            nc.gpsimd.memset(m_bd[:, :], 0.0)
            nc.gpsimd.memset(average[:, :, :], 0.0).then_inc(S["zeros"], 1)
            pool.wait_ge(S["zeros"], 1)
            for k in range(1 - G, G):
                ins = nc.gpsimd.affine_select(out=average[:, :, :], in_=average[:, :, :], compare_op=ALU.not_equal,
                                              fill=1.0 / G, base=C * k, pattern=[[-C, G], [-1, C]],
                                              channel_multiplier=1)
                ins.then_inc(S["average_set"], 1)
                pool.wait_ge(S["average_set"], k + G)
            nc.gpsimd.memset(r_tile[:, :], 0.0).then_inc(S["zeros"], 1)
            for q in range(1, Q):
                pool.wait_ge(S["ln_rstd"], q + 1)
                pool.wait_ge(S["ln_squared"], q + 1)
                nc.gpsimd.tensor_tensor(y[:, q, :, :], y[:, q, :, :],
                                        stat[:, 2, q, :].unsqueeze(2).broadcast_to([P, C, C]),
                                        ALU.mult).then_inc(S["y_ready"], 1)
            nc.gpsimd.memset(rv_bd[:, :, :], 0.0).then_inc(S["zeros"], 1)
            nc.gpsimd.memset(ones[:, :], 1.0).then_inc(S["ones_set"], 1)
            nc.gpsimd.memset(warm[:, :, :, :, :], 0.0).then_inc(S["warm_zero"], 1)
            for q in range(Q):
                pool.wait_ge(S["score_max"], q + 1)
                nc.gpsimd.tensor_tensor(att[:, q, :, :], att[:, q, :, :],
                                        soft[:, 0, q, :].unsqueeze(2).broadcast_to([P, C, C]),
                                        ALU.subtract).then_inc(S["score_shifted"], 1)

            def centre(k):
                pool.wait_ge(S["t_mean"], k + 1)
                nc.gpsimd.tensor_tensor(unit(x2n, k), unit(x2, k), stat2[:, 0, k, :].unsqueeze(2).broadcast_to([P, C // 2, C]),
                                        ALU.subtract).then_inc(S["t_centred"], 1)

            def scale(k):
                pool.wait_ge(S["t_rstd"], k + 1)
                pool.wait_ge(S["t_squared"], k + 1)
                nc.gpsimd.tensor_tensor(unit(x2n, k), unit(x2n, k), stat2[:, 2, k, :].unsqueeze(2).broadcast_to([P, C // 2, C]),
                                        ALU.mult).then_inc(S["t_norm"], 1)

            for q in range(Q):
                if q < Q - 1:
                    centre(2 * q)
                    centre(2 * q + 1)
                scale(2 * q)
                scale(2 * q + 1)

            for n, (row, k) in enumerate(PIECES):
                for r in range(0, STREAMS, 2):
                    pool.wait_ge(S["turned_back"], STREAMS * n + r + 1)
                    add_back(nc.gpsimd, row, k, r).then_inc(S["added_pool"], 1)

        @block.scalar
        def _(act):
            def u_half(q, k):
                act.wait_ge(S["u_product"], 2 * q + k + 1)
                nc.scalar.copy(u_tile[:, IMG * q + BANK * k:IMG * q + BANK * (k + 1)], bank(k)).then_inc(S["u_half"], 1)

            for q in range(Q):
                act.wait_ge(S["ln_centred"], q + 1)
                if q >= 2:
                    act.wait_ge(S["ln_sum2"], q - 1)
                nc.scalar.activation(square[:, q % 2, :], y[:, q, :, :].rearrange("p i j -> p (i j)"),
                                     ACT.Square).then_inc(S["ln_squared"], 1)
                if q == 0:
                    act.wait_ge(S["m_product"], 1)
                    act.wait_ge(S["zeros"], 1)
                    for g in range(G):
                        p = slice(C * g, C * (g + 1))
                        nc.scalar.mul(m_bd[p, p], ps[p, 6, 0:C], 1.0 / d).then_inc(S["m_set"], 1)
                act.wait_ge(S["ln_var"], q + 1)
                nc.scalar.activation(stat[:, 2, q, :], stat[:, 1, q, :], ACT.Sqrt).then_inc(S["ln_std"], 1)
                if q == 1:
                    u_half(0, 0)
                    u_half(0, 1)
            act.wait_ge(S["r_product"], 1)
            act.wait_ge(S["zeros"], 2)
            for g in range(G):
                p = slice(C * g, C * (g + 1))
                nc.scalar.copy(r_bd[p, :, p], ps[p, 6:8, :].rearrange("p b (h i) -> p i (b h)", i=C)
                               ).then_inc(S["r_set"], 1)
            for q in range(1, Q):
                u_half(q, 0)
                u_half(q, 1)
            for b in range(BLOCKS):
                act.wait_ge(S["rel_product"], b + 1)
                nc.scalar.copy(rel[:, :, ROWS * b:ROWS * (b + 1), :],
                               bank(6 + b % 2).rearrange("p (i q j) -> p q i j", i=ROWS, q=Q)).then_inc(S["rel_ready"], 1)
            for q in range(Q):
                act.wait_ge(S["score_shifted"], q + 1)
                nc.scalar.activation(att[:, q, :, :].rearrange("p i j -> p (i j)"),
                                     att[:, q, :, :].rearrange("p i j -> p (i j)"), ACT.Exp).then_inc(S["score_exp"], 1)
            def wsum_out(q, jh):
                act.wait_ge(S["wsum_product"], 2 * q + jh + 1)
                nc.scalar.copy(wsum[:, q, :, 16 * jh:16 * (jh + 1)],
                               bank(jh).rearrange("p (j i) -> p i j", i=C)).then_inc(S["wsum_half"], 1)

            def t_square(k):
                if k < UNITS - 2:
                    act.wait_ge(S["t_centred"], k + 1)
                else:
                    act.wait_ge(S["t_centred_dve"], k - (UNITS - 2) + 1)
                if k >= 2:
                    act.wait_ge(S["t_sum2"], k - 1)
                nc.scalar.activation(square[:, k % 2, 0:BANK].rearrange("p (i j) -> p i j", j=C),
                                     unit(x2n, k), ACT.Square).then_inc(S["t_squared"], 1)

            def t_std(k):
                act.wait_ge(S["t_var"], k + 1)
                nc.scalar.activation(stat2[:, 2, k, :], stat2[:, 1, k, :], ACT.Sqrt).then_inc(S["t_std"], 1)

            def wx_out(k):
                act.wait_ge(S["wx_product"], k + 1)
                nc.scalar.copy(wx_rows(k), bank(WX_BANK[k % 2]).rearrange("p (i c) -> p i c", c=C)).then_inc(S["wx_ready"], 1)

            wsum_out(0, 0)
            wsum_out(0, 1)
            for q in range(Q):
                if q + 1 < Q:
                    wsum_out(q + 1, 0)
                t_square(2 * q)
                t_square(2 * q + 1)
                t_std(2 * q)
                t_std(2 * q + 1)
                if q + 1 < Q:
                    wsum_out(q + 1, 1)
                if q >= 1:
                    wx_out(2 * q - 2)
                    wx_out(2 * q - 1)
            wx_out(UNITS - 2)
            wx_out(UNITS - 1)
            act.wait_ge(S["bn_var_s"], 1)
            nc.scalar.activation(bnv[:, 6:7], bnv[:, 5:6], ACT.Sqrt).then_inc(S["bn_std"], 1)

            for t in range(ROUNDS):
                for r in range(STREAMS):
                    if t == 0:
                        act.wait_ge(S["seeded"], r + 1)
                        act.wait_ge(S["warm_zero"], 1)
                    else:
                        act.wait_ge(S["preact"], STREAMS * (t - 1) + r + 1)
                    nc.scalar.activation(state_out(t, r), rec_slot(t, r).rearrange("p (q c) -> p q c", q=Q),
                                         ACT.Sigmoid).then_inc(S["state"], 1)

            act.wait_ge(S["flag"], 1)
            repeat = act.value_load(repeat_flag[0:1, 0:1], min_val=0, max_val=1)
            with act.If(repeat == 1):
                with act.Fori(0, SEGMENTS - 1) as n:
                    for s in range(SEG):
                        for r in range(STREAMS):
                            act.wait_ge(S["f_preact"], n * (SEG * STREAMS) + (STREAMS * s + r + 1))
                            nc.scalar.activation(states[:, SEG * r + s, :, :],
                                                 rec_slot(WARM + s, r).rearrange("p (q c) -> p q c", q=Q),
                                                 ACT.Sigmoid).then_inc(S["f_state"], 1)

        @block.vector
        def _(dve):
            def spread_out(k, src, gate, factor):
                nc.vector.tensor_scalar(spread[:, k, :].rearrange("p (g c) -> p g c", g=G),
                                        src.unsqueeze(1).broadcast_to([C, G, C]), gate, factor,
                                        ALU.mult, ALU.mult).then_inc(S["w_spread"], 1)

            def setup_weights():
                dve.wait_ge(S["wqk_in"], 32)
                dve.wait_ge(S["gates_in"], 32)
                spread_out(0, wsmall[0:C, 4, :], gates[0:C, 0:1], 1.0 / d)
                spread_out(1, wsmall[0:C, 3, :], gates[0:C, 1:2], 1.0 / d)

            def setup_turned():
                dve.wait_ge(S["gates2_in"], 32)
                dve.wait_ge(S["average_set"], 2 * G - 1)
                spread_out(2, average[0:C, 0, :], gates[0:C, 3:4], float(G))
                dve.wait_ge(S["w_in"], 16 * 3)
                nc.vector.transpose(wturned[:, :, :], wsmall[:, 0:3, :]).then_inc(S["turned"], 1)
                dve.wait_ge(S["turned"], 1)
                dve.wait_ge(S["zeros"], 1)
                for g in range(G):
                    p = slice(C * g, C * (g + 1))
                    nc.vector.tensor_scalar(w_bd[p, 0, p], wturned[p, 0, :], gates[p, 2:3], None,
                                            ALU.mult).then_inc(S["w_set"], 1)
                    nc.vector.tensor_copy(w_bd[p, 1:3, p], wturned[p, 1:3, :]).then_inc(S["w_set"], 1)
                dve.wait_ge(S["rv_in"], 16)
                nc.vector.transpose(rv_t[:, :, :], r_in[:, 2, :].rearrange("p (h i) -> p i h", h=C)
                                    ).then_inc(S["rv_turned"], 1)

            def set_rv():
                dve.wait_ge(S["rv_product"], 1)
                dve.wait_ge(S["zeros"], 3)
                for g in range(G):
                    p = slice(C * g, C * (g + 1))
                    nc.vector.tensor_copy(rv_bd[p, :, p], ps[p, 4:6, :].rearrange("p b (i c) -> p (b i) c", c=C)
                                          ).then_inc(S["rv_set"], 1)

            def ln_centre(q):
                dve.wait_ge(S[f"x_in{q}"], 16)
                nc.vector.tensor_reduce(stat[:, 1, q, :], xin[:, q, :, :], AX_X, ALU.add).then_inc(S["ln_sum"], 1)
                dve.wait_ge(S["ln_sum"], q + 1)
                nc.vector.tensor_scalar(stat[:, 0, q, :], stat[:, 1, q, :], 1.0 / C, None, ALU.mult).then_inc(S["ln_mean"], 1)
                dve.wait_ge(S["ln_mean"], q + 1)
                nc.vector.tensor_tensor(y[:, q, :, :], xin[:, q, :, :],
                                        stat[:, 0, q, :].unsqueeze(2).broadcast_to([P, C, C]),
                                        ALU.subtract).then_inc(S["ln_centred"], 1)

            def ln_var(q):
                dve.wait_ge(S["ln_squared"], q + 1)
                nc.vector.tensor_reduce(stat[:, 0, q, :], square[:, q % 2, :].rearrange("p (i j) -> p i j", i=C),
                                        AX_X, ALU.add).then_inc(S["ln_sum2"], 1)
                dve.wait_ge(S["ln_sum2"], q + 1)
                nc.vector.tensor_scalar(stat[:, 1, q, :], stat[:, 0, q, :], 1.0 / C, LN1_EPS,
                                        ALU.mult, ALU.add).then_inc(S["ln_var"], 1)

            def ln_rstd(q):
                dve.wait_ge(S["ln_std"], q + 1)
                nc.vector.reciprocal(stat[:, 2, q, :], stat[:, 2, q, :]).then_inc(S["ln_rstd"], 1)

            for t in range(Q + 1):
                if t < Q:
                    ln_centre(t)
                if t >= 1:
                    ln_var(t - 1)
                    ln_rstd(t - 1)
                if t == 1:
                    dve.wait_ge(S["ln_rstd"], 1)
                    nc.vector.tensor_tensor(y[:, 0, :, :], y[:, 0, :, :],
                                            stat[:, 2, 0, :].unsqueeze(2).broadcast_to([P, C, C]),
                                            ALU.mult).then_inc(S["y0_ready"], 1)
                    setup_weights()
            setup_turned()
            for q in range(Q):
                wait_y(dve, q)
                nc.vector.transpose(y_t[:, q, :, :], y[:, q, :, :].rearrange("p h j -> p j h")).then_inc(S["y_turned"], 1)

            set_rv()

            def score_max(q):
                dve.wait_ge(S["score_product"], 2 * q + 2)
                dve.wait_ge(S["rel_ready"], BLOCKS)
                nc.vector.tensor_tensor(att[:, q, :, :],
                                        ps[:, half_scores(q, 0):half_scores(q, 0) + 2, :]
                                        .rearrange("p b (j i) -> p i (b j)", i=C),
                                        rel[:, q, :, :], ALU.add).then_inc(S["score_sum"], 1)
                dve.wait_ge(S["score_sum"], q + 1)
                nc.vector.tensor_reduce(soft[:, 0, q, :], att[:, q, :, :], AX_X, ALU.max).then_inc(S["score_max"], 1)

            def weights(q):
                dve.wait_ge(S["score_exp"], q + 1)
                nc.vector.tensor_reduce(soft[:, 1, q, :], att[:, q, :, :], AX_X, ALU.add).then_inc(S["weight_sum"], 1)
                dve.wait_ge(S["weight_sum"], q + 1)
                nc.vector.reciprocal(soft[:, 1, q, :], soft[:, 1, q, :]).then_inc(S["weight_recip"], 1)
                dve.wait_ge(S["weight_recip"], q + 1)
                nc.vector.tensor_tensor(att[:, q, :, :], att[:, q, :, :],
                                        soft[:, 1, q, :].unsqueeze(2).broadcast_to([P, C, C]),
                                        ALU.mult).then_inc(S["weights"], 1)

            for t in range(Q + 1):
                if t < Q:
                    score_max(t)
                if t >= 1:
                    weights(t - 1)

            for b in range(BLOCKS):
                rows = slice(ROWS * b, ROWS * (b + 1))
                dve.wait_ge(S["relv_product"], b + 1)
                nc.vector.tensor_tensor(x2[:, :, rows, :],
                                        bank(ATT_BANK[b % 4]).rearrange("p (q i j) -> p q i j", q=Q, i=ROWS),
                                        xin[:, :, rows, :], ALU.add).then_inc(S["x2_part"], 1)
            dve.wait_ge(S["x2_part"], BLOCKS)

            def residual(k):
                dve.wait_ge(S["proj_product"], k + 1)
                nc.vector.tensor_tensor(unit(x2, k), bank(PROJ_BANK[k]).rearrange("p (i j) -> p i j", j=C),
                                        unit(x2, k), ALU.add).then_inc(S["x2_ready"], 1)
                dve.wait_ge(S["x2_ready"], k + 1)
                nc.vector.tensor_reduce(stat2[:, 1, k, :], unit(x2, k), AX_X, ALU.add).then_inc(S["t_sum"], 1)
                dve.wait_ge(S["t_sum"], k + 1)
                nc.vector.tensor_scalar(stat2[:, 0, k, :], stat2[:, 1, k, :], 1.0 / C, None, ALU.mult).then_inc(S["t_mean"], 1)
                if k >= UNITS - 2:
                    dve.wait_ge(S["t_mean"], k + 1)
                    nc.vector.tensor_tensor(unit(x2n, k), unit(x2, k),
                                            stat2[:, 0, k, :].unsqueeze(2).broadcast_to([P, C // 2, C]),
                                            ALU.subtract).then_inc(S["t_centred_dve"], 1)

            def t_var(k):
                dve.wait_ge(S["t_squared"], k + 1)
                nc.vector.tensor_reduce(stat2[:, 0, k, :], square[:, k % 2, 0:BANK].rearrange("p (m j) -> p m j", j=C),
                                        AX_X, ALU.add).then_inc(S["t_sum2"], 1)
                dve.wait_ge(S["t_sum2"], k + 1)
                nc.vector.tensor_scalar(stat2[:, 1, k, :], stat2[:, 0, k, :], 1.0 / C, LN2_EPS,
                                        ALU.mult, ALU.add).then_inc(S["t_var"], 1)

            def t_rstd(k):
                dve.wait_ge(S["t_std"], k + 1)
                nc.vector.reciprocal(stat2[:, 2, k, :], stat2[:, 2, k, :]).then_inc(S["t_rstd"], 1)

            def t_turn(k):
                dve.wait_ge(S["t_norm"], k + 1)
                nc.vector.transpose(tokens[:, 16 * (k % 2):16 * (k % 2 + 1), k // 2, :], unit(x2n, k)
                                    ).then_inc(S["t_turned"], 1)

            def bn_part(k):
                dve.wait_ge(S["wx_ready"], k + 1)
                nc.vector.bn_stats(bn[:, k, :], wx_rows(k)).then_inc(S["bn_part"], 1)

            for q in range(Q):
                for stage in (residual, t_var, t_rstd, t_turn):
                    stage(2 * q)
                    stage(2 * q + 1)
                if q >= 1:
                    bn_part(2 * q - 2)
                    bn_part(2 * q - 1)
            nc.vector.memset(ps[:, 7, 0:2], 0.0).then_inc(S["bn_zero"], 1)
            bn_part(UNITS - 2)
            bn_part(UNITS - 1)

            gmean, gvar, mean, off, spr, var, std, scl, ms, shift = (bnv[:, k:k + 1] for k in range(10))
            dve.wait_ge(S["bn_part"], BLOCKS)
            nc.vector.bn_aggr(bnv[:, 0:2], bn[:, :, :]).then_inc(S["bn_group"], 1)
            dve.wait_ge(S["bn_mean"], 1)
            nc.vector.tensor_copy(mean, ps[:, 7, 0:1]).then_inc(S["bn_mean_s"], 1)
            dve.wait_ge(S["bn_mean_s"], 1)
            nc.vector.tensor_tensor(off, gmean, mean, ALU.subtract).then_inc(S["bn_off"], 1)
            dve.wait_ge(S["bn_off"], 1)
            nc.vector.scalar_tensor_tensor(out=spr, in0=off, scalar=off, in1=gvar, op0=ALU.mult,
                                           op1=ALU.add).then_inc(S["bn_spread"], 1)
            dve.wait_ge(S["bn_var"], 1)
            nc.vector.tensor_scalar(var, ps[:, 7, 1:2], BN_EPS, None, ALU.add).then_inc(S["bn_var_s"], 1)
            dve.wait_ge(S["bn_std"], 1)
            dve.wait_ge(S["affine_in"], 32)
            nc.vector.reciprocal(std, std).then_inc(S["bn_rstd"], 1)
            dve.wait_ge(S["bn_rstd"], 1)
            nc.vector.tensor_tensor(scl, std, affine[:, 0:1], ALU.mult).then_inc(S["bn_scale"], 1)
            dve.wait_ge(S["bn_scale"], 1)
            nc.vector.tensor_tensor(ms, mean, scl, ALU.mult).then_inc(S["bn_ms"], 1)
            dve.wait_ge(S["bn_ms"], 1)
            nc.vector.tensor_tensor(shift, affine[:, 1:2], ms, ALU.subtract).then_inc(S["bn_shift"], 1)
            dve.wait_ge(S["bn_shift"], 1)

            def seed(n, r):
                t, k = SEEDS[n]
                row, at = SEG * r + round_row(t), round_row(t) % ROWS
                return nc.vector.tensor_scalar(bank(rec_bank(t, r))[:, P * at:P * (at + k)],
                                               wx[:, row:row + k, :].rearrange("p i m -> p (i m)"),
                                               scl, shift, ALU.mult, ALU.add)

            def seeds(n):
                for r in range(STREAMS):
                    if n >= 2:
                        dve.wait_ge(S["state"], STREAMS * (SEEDS[n - 1][0] - 1) + r + 1)
                    seed(n, r).then_inc(S["seeded"], 1)

            def finish(n):
                row, k = PIECES[n]
                for r in range(STREAMS):
                    dve.wait_ge(S["state"], STREAMS * (WARM + row + k - 1) + r + 1)
                    if n >= 1:
                        if r % 2:
                            dve.wait_ge(S["added_dve"], 2 * (n - 1) + r // 2 + 1)
                        else:
                            dve.wait_ge(S["added_pool"], 2 * (n - 1) + r // 2 + 1)
                    turn_back(row, k, r).then_inc(S["turned_back"], 1)
                    if r % 2:
                        dve.wait_ge(S["turned_back"], STREAMS * n + r + 1)
                        add_back(nc.vector, row, k, r).then_inc(S["added_dve"], 1)

            seeds(0)
            seeds(1)
            for n in range(2, len(SEEDS)):
                seeds(n)
            for n in range(len(PIECES)):
                finish(n)

            dve.wait_ge(S["state"], STREAMS * ROUNDS)
            nc.vector.tensor_tensor(diff[:, 0, :].rearrange("p (r q c) -> p r q c", r=STREAMS, q=Q),
                                    states[:, SEG - 1::SEG, :, :], warm[:, FINAL_SIDE, :, :, 1:C + 1],
                                    ALU.subtract).then_inc(S["diff_d"], 1)
            dve.wait_ge(S["diff_d"], 1)
            nc.vector.tensor_tensor_reduce(diff[:, 1, :], diff[:, 0, :], diff[:, 0, :], 1.0, 0.0,
                                           ALU.mult, ALU.add, diffsum[:, :]).then_inc(S["diff_sum"], 1)
            dve.wait_ge(S["diff_sum"], 1)
            nc.vector.tensor_scalar(agreed[:, :], diffsum[:, :], AGREE * AGREE, None, ALU.is_le).then_inc(S["agreed"], 1)
            dve.wait_ge(S["agree_count"], 1)
            nc.vector.tensor_scalar(repeat_flag[:, :], ps[0:1, 0, 0:1], float(P), None,
                                    ALU.is_lt).then_inc(S["flag"], 1)
            dve.wait_ge(S["flag"], 1)
            repeat = dve.value_load(repeat_flag[0:1, 0:1], min_val=0, max_val=1)
            with dve.If(repeat == 1):
                PASS = SEG * STREAMS
                dve.wait_ge(S["f_marked"], 1)
                with dve.Fori(0, SEGMENTS - 1) as n:
                    nc.vector.tensor_copy(warm[:, FINAL_SIDE, :, :, 1:C + 1], states[:, SEG - 1::SEG, :, :]).then_inc(S["f_start"], 1)
                    for h in range(GROUPS):
                        for r in range(STREAMS):
                            seed(len(SEEDS) - GROUPS + h, r).then_inc(S["f_seeded"], 1)
                    dve.wait_ge(S["f_state"], n * PASS + PASS)
                dve.wait_ge(S["stored"], STORED)
                for h in range(GROUPS):
                    for r in range(STREAMS):
                        n = GROUPS * (STREAMS * h + r)
                        turn_back(ROWS * h, ROWS, r).then_inc(S["f_turned"], 1)
                        dve.wait_ge(S["f_turned"], n + 1)
                        add_back(nc.vector, ROWS * h, ROWS, r).then_inc(S["f_turned"], 1)
                        dve.wait_ge(S["f_turned"], n + 2)

        @block.tensor
        def _(pe):
            pe.wait_ge(S["wqk_in"], 32)
            for g in range(G):
                p = slice(C * g, C * (g + 1))
                ins = nc.tensor.matmul(ps[p, 6, 0:C], wsmall[p, 3, :], wsmall[p, 4, :], start=True, stop=True)
            ins.then_inc(S["m_product"], 1)
            pe.wait_ge(S["m_set"], G)

            def project_u(q):
                for k in range(2):
                    if q >= 1:
                        pe.wait_ge(S["u_half"], 2 * (q - 1) + k + 1)
                    nc.tensor.matmul(bank(k), m_bd[:, :], y[:, q, 16 * k:16 * (k + 1), :].rearrange("p i j -> p (i j)"),
                                     start=True, stop=True).then_inc(S["u_product"], 1)

            def scores(q):
                pe.wait_ge(S["u_half"], 2 * q + 2)
                if q >= 2:
                    pe.wait_ge(S["score_sum"], q - 1)
                for j in range(C):
                    for g in range(G):
                        p = slice(C * g, C * (g + 1))
                        ins = nc.tensor.matmul(ps[p, half_scores(q, j // 16), C * (j % 16):C * (j % 16 + 1)],
                                               u[p, q, :, j], y[p, q, :, j], start=True, stop=True)
                    if j % 16 == 15:
                        ins.then_inc(S["score_product"], 1)

            def relative_factor():
                pe.wait_ge(S["w_spread"], 2)
                pe.wait_ge(S["r_in_s"], 16 * 2)
                for k in range(2):
                    cols = slice(BANK * k, BANK * (k + 1))
                    nc.tensor.matmul(bank(6 + k), spread[:, 0, :], r_in[:, 0, cols], start=True, stop=False)
                    ins = nc.tensor.matmul(bank(6 + k), spread[:, 1, :], r_in[:, 1, cols], start=False, stop=True)
                ins.then_inc(S["r_product"], 1)

            def relative_values():
                pe.wait_ge(S["w_spread"], 3)
                pe.wait_ge(S["rv_turned"], 1)
                for k in range(2):
                    ins = nc.tensor.matmul(bank(4 + k), spread[:, 2, :],
                                           rv_t[:, 16 * k:16 * (k + 1), :].rearrange("p i c -> p (i c)"),
                                           start=True, stop=True)
                ins.then_inc(S["rv_product"], 1)

            for q in range(Q):
                wait_y(pe, q)
                project_u(q)
                if q == 0:
                    relative_factor()
                    scores(0)
            relative_values()
            pe.wait_ge(S["r_set"], G)
            for b in range(BLOCKS):
                if b >= 2:
                    pe.wait_ge(S["rel_ready"], b - 1)
                for k in range(ROWS):
                    ins = nc.tensor.matmul(bank(6 + b % 2)[:, P * k:P * (k + 1)], r_bd[:, ROWS * b + k, :],
                                           y[:, :, ROWS * b + k, :], start=True, stop=True)
                ins.then_inc(S["rel_product"], 1)
            pe.wait_ge(S["rv_set"], G)
            for q in range(1, Q):
                scores(q)

            def weighted_sums(q, jh):
                pe.wait_ge(S["weights"], q + 1)
                pe.wait_ge(S["y_turned"], q + 1)
                if q >= 1:
                    pe.wait_ge(S["wsum_half"], 2 * (q - 1) + jh + 1)
                for j in range(16 * jh, 16 * (jh + 1)):
                    for g in range(G):
                        p = slice(C * g, C * (g + 1))
                        ins = nc.tensor.matmul(ps[p, jh, C * (j % 16):C * (j % 16 + 1)],
                                               y_t[p, q, j, :], att[p, q, :, j], start=True, stop=True)
                ins.then_inc(S["wsum_product"], 1)

            def value_rows(b):
                if b < 4:
                    pe.wait_ge(S["score_sum"], Q)
                else:
                    pe.wait_ge(S["x2_part"], b - 3)
                rows = bank(ATT_BANK[b % 4]).rearrange("p (q i j) -> p q i j", q=Q, i=ROWS)
                for k in range(ROWS):
                    ins = nc.tensor.matmul(rows[:, :, k, :], rv_bd[:, ROWS * b + k, :], att[:, :, ROWS * b + k, :],
                                           start=(k == 0), stop=True, skip_group_check=True)
                ins.then_inc(S["relv_product"], 1)

            def project_values(k):
                pe.wait_ge(S["wsum_half"], 2 * (k // 2) + 2)
                if k in (2, 3, 4, 5):
                    pe.wait_ge(S["x2_ready"], k - 1)
                nc.tensor.matmul(bank(PROJ_BANK[k]), w_bd[:, 0, :], unit(wsum, k).rearrange("p i j -> p (i j)"),
                                 start=True, stop=True).then_inc(S["proj_product"], 1)

            def project_wx(k):
                pe.wait_ge(S["t_turned"], k + 1)
                if k >= 2:
                    pe.wait_ge(S["wx_ready"], k - 1)
                nc.tensor.matmul(bank(WX_BANK[k % 2]), w_bd[:, 1, :],
                                 tokens[:, 16 * (k % 2):16 * (k % 2 + 1), k // 2, :],
                                 start=True, stop=True).then_inc(S["wx_product"], 1)

            weighted_sums(0, 0)
            weighted_sums(0, 1)
            pe.wait_ge(S["weights"], Q)
            for b in range(BLOCKS):
                value_rows(b)
            pe.wait_ge(S["w_set"], 2 * G)
            pe.wait_ge(S["rel_ready"], BLOCKS)
            pe.wait_ge(S["x2_part"], BLOCKS)
            for q in range(1, Q):
                weighted_sums(q, 0)
                project_values(2 * q - 2)
                project_values(2 * q - 1)
                weighted_sums(q, 1)
                if q >= 2:
                    project_wx(2 * q - 4)
                    project_wx(2 * q - 3)
            for k in (UNITS - 2, UNITS - 1):
                project_values(k)
            for k in range(UNITS - 4, UNITS):
                project_wx(k)

            pe.wait_ge(S["bn_zero"], 1)
            pe.wait_ge(S["bn_group"], 1)
            avg = average[:, :, :].rearrange("p g c -> p (g c)")
            nc.tensor.matmul(ps[:, 7, 0:1], avg, bnv[:, 0:1], start=False, stop=True,
                             skip_group_check=True).then_inc(S["bn_mean"], 1)
            pe.wait_ge(S["bn_spread"], 1)
            nc.tensor.matmul(ps[:, 7, 1:2], avg, bnv[:, 4:5], start=False, stop=True,
                             skip_group_check=True).then_inc(S["bn_var"], 1)

            for t in range(1, ROUNDS):
                for r in range(STREAMS):
                    if t == 1 or SEED_OF[t] > SEED_OF[t - 1]:
                        pe.wait_ge(S["seeded"], STREAMS * SEED_OF[t] + r + 1)
                    src = (r - 1) % STREAMS if round_row(t) == 0 else r
                    pe.wait_ge(S["state"], STREAMS * (t - 1) + src + 1)
                    nc.tensor.matmul(rec_slot(t, r), w_bd[:, 2, :], state_in(t, r), start=False, stop=True,
                                     skip_group_check=True).then_inc(S["preact"], 1)

            pe.wait_ge(S["agreed"], 1)
            nc.tensor.matmul(ps[0:1, 0, 0:1], agreed[:, :], ones[:, :], start=True, stop=True).then_inc(S["agree_count"], 1)
            pe.wait_ge(S["flag"], 1)
            repeat = pe.value_load(repeat_flag[0:1, 0:1], min_val=0, max_val=1)
            with pe.If(repeat == 1):
                nc.tensor.matmul(bank(0), w_bd[:, 2, :], wx[:, 0:ROWS, :].rearrange("p i m -> p (i m)"),
                                 start=True, stop=True).then_inc(S["f_marked"], 1)
                with pe.Fori(0, SEGMENTS - 1) as n:
                    pe.wait_ge(S["f_start"], n + 1)
                    for s in range(SEG):
                        for r in range(STREAMS):
                            if s % ROWS == 0:
                                pe.wait_ge(S["f_seeded"], n * (GROUPS * STREAMS) + (STREAMS * (s // ROWS) + r + 1))
                            if s > 0:
                                pe.wait_ge(S["f_state"], n * (SEG * STREAMS) + (STREAMS * (s - 1) + r + 1))
                            nc.tensor.matmul(rec_slot(WARM + s, r), w_bd[:, 2, :],
                                             start_state(FINAL_SIDE, r) if s == 0 else states[:, SEG * r + s - 1, :, :],
                                             start=False, stop=True, skip_group_check=True).then_inc(S["f_preact"], 1)


_INS = ["x", "L0_conv_Wq", "L0_conv_Wk", "L0_conv_Wv", "L0_conv_rq", "L0_conv_rk", "L0_conv_rv", "L0_conv_Gq",
        "L0_conv_Gk", "L0_conv_Gv1", "L0_conv_Gv2", "L0_ffn_W", "L0_ffn_V", "L0_ffn_gamma", "L0_ffn_beta"]
_OUTS = [((16, 32, 32, 32), "float32")]


def kernel(**inputs):
    import numpy as _np
    import concourse.bacc as _bacc
    from concourse import mybir as _mybir
    from concourse.bass_utils import run_bass_kernel_spmd as _run

    nc = _bacc.Bacc("TRN2", target_bir_lowering=False, num_devices=1)
    arrays, args = {}, []
    for name in _INS:
        a = _np.ascontiguousarray(inputs[name])
        arrays[f"in_{name}_dram"] = a
        args.append(nc.dram_tensor(f"in_{name}_dram", a.shape, _mybir.dt.from_np(a.dtype), kind="ExternalInput").ap())
    for i, (shape, dtype) in enumerate(_OUTS):
        dt = _mybir.dt.from_np(_np.dtype(dtype))
        args.append(nc.dram_tensor(f"out_{i}_dram", shape, dt, kind="ExternalOutput").ap())
    metaformer_kernel(nc, *args)
    r = _run(nc, [arrays], core_ids=[0])
    got = tuple(r.results[0][f"out_{i}_dram"] for i in range(len(_OUTS)))
    return got[0]
```

```python
from contextlib import ExitStack

import concourse.bass as bass
from concourse import mybir

P = 128
G = 4
Q = 4
C = 32
COLS = Q * C * C
IMG = C * C
BANK = 512
ROWS = 4
BLOCKS = C // ROWS
STREAMS = 4
SEG = C // STREAMS
GROUPS = SEG // ROWS
UNITS = 2 * Q
WARM = 10
ROUNDS = WARM + SEG
SEGMENTS = C * STREAMS
LN_PARTS = [(0, 0, 16), (0, 16, 16), (1, 0, 32), (2, 0, 32), (3, 0, 32)]
POOL_SCALED = 3
ON_DVE = [(0, 3), (1, 1), (1, 3), (2, 1), (2, 3)]
PIECES = [(0, 4), (4, 2), (6, 2)]
STORES = [(0, 0, 4), (2, 4, 4)]
AGREE = 2.0 ** -18
LN1_EPS = 1e-6
LN2_EPS = 1e-5
BN_EPS = 1e-5

ALU = mybir.AluOpType
ACT = mybir.ActivationFunctionType
F32 = mybir.dt.float32
I32 = mybir.dt.int32
AX_X = mybir.AxisListType.X


def metaformer_kernel(nc, x, Wq, Wk, Wv, rq, rk, rv, Gq, Gk, Gv1, Gv2, W, V, gamma, beta, out):
    d = float(C) ** 0.5
    x_dram = x.rearrange("(q g) c i j -> q (g c) (i j)", g=G)
    out_dram = out.rearrange("(q g) c i j -> (g c) q (i j)", g=G)

    with ExitStack() as ctx:
        def sb(name, shape, dt=F32):
            return ctx.enter_context(nc.sbuf_tensor(name, shape, dt))

        def sem(name):
            return ctx.enter_context(nc.semaphore(name))

        xin = sb("xin", [P, Q, C, C])
        y = sb("y", [P, Q, C, C])
        u_tile = sb("u_tile", [P, COLS])
        yt_tile = sb("yt_tile", [P, COLS])
        bias_tile = sb("bias_tile", [P, COLS])
        att = sb("att", [P, Q, C, C])
        r_tile = sb("r_tile", [P, COLS])
        rv_bd = sb("rv_bd", [P, C, P])
        x2 = sb("x2", [P, Q, C, C])
        x2n = sb("x2n", [P, Q, C, C])
        wx_q = bias_tile[:, :].rearrange("p (i q c) -> p i q c", i=C, q=Q)
        u = u_tile[:, :].rearrange("p (q h j) -> p q h j", q=Q, h=C)
        tokens = u_tile[:, :].rearrange("p (i q c) -> p i q c", i=C, q=Q)
        v_t = yt_tile[:, :].rearrange("p (q j c) -> p q j c", q=Q, j=C)
        wx = bias_tile[:, :].rearrange("p (i m) -> p i m", i=C)
        rel = bias_tile[:, :].rearrange("p (q i j) -> p q i j", q=Q, i=C)
        states = yt_tile[:, :].rearrange("p (i q c) -> p i q c", i=C, q=Q)
        r_bd = r_tile[:, :].rearrange("p (i m) -> p i m", i=C)
        values = r_tile[:, :].rearrange("p (q h j) -> p q h j", q=Q, h=C)
        result = y

        square = sb("square", [P, 2, IMG])
        stat = sb("stat", [P, 3, Q, C])
        soft = sb("soft", [P, 2, Q, C])
        stat2 = sb("stat2", [P, 3, UNITS, C // 2])
        back = xin[:, :, :, :].rearrange("p q i j -> p (q i j)")
        warm = sb("warm", [P, 2, STREAMS, Q, C + 1])

        wsmall = sb("wsmall", [P, 5, C])
        wturned = sb("wturned", [P, 3, C])
        w_bd = sb("w_bd", [P, 3, P])
        m_bd = sb("m_bd", [P, P])
        r_in = sb("r_in", [2 * C, IMG])
        rv_in = sb("rv_in", [C, IMG])
        rv_t = sb("rv_t", [C, C, C])
        spread = sb("spread", [2 * C, P])
        spread_v = sb("spread_v", [C, P])
        gates = sb("gates", [P, 4])
        affine = sb("affine", [P, 2])
        average = sb("average", [P, G, C])
        ones = sb("ones", [P, 1])
        bn = sb("bn", [P, BLOCKS, 6])
        bnv = sb("bnv", [P, 8])
        std, scl, shift = (bnv[:, k:k + 1] for k in range(5, 8))
        bn_eps = sb("bn_eps", [P, 1])
        table_load = sb("table_load", [P, 1])
        diff = square[:, :, :].rearrange("p b (k m) -> p (b k) m", k=2)
        agreed = sb("agreed", [P, 1])
        diffsum = sb("diffsum", [P, 1])
        repeat_flag = sb("repeat_flag", [1, 1], I32)

        ps = ctx.enter_context(nc.psum_tensor("ps", [P, 8, BANK], F32))

        names = """x_in0 x_in1 x_in2 x_in3 x_in4 wqk_in w_in r_in_s rv_in gates_in gates2_in affine_in zeros average_set ones_set turned w_spread
        m_product m_set w_set r_product r_set rv_turned rv_product rv_set
        ln_sum ln_mean ln_centred ln_squared ln_sum2 ln_var ln_std ln_rstd y_ready_dve y_ready_pool v_turned
        u_product u_half rel_product rel_ready score_product score_sum score_max score_shifted
        score_exp weight_sum weight_recip weights wsum_product value_product value_half
        relv_product x2_part t_centred_dve x2_ready t_sum t_mean t_centred t_squared t_sum2 t_var t_std t_rstd t_norm t_norm_dve
        t_turned wx_product wx_ready bn_part bn_group bn_zero bn_mean bn_mean_s bn_off bn_spread
        marked eps_set bn_var bn_std bn_rstd bn_scale bn_shift seeded_act
        warm_zero warmed seeded preact state turned_back added_dve added_pool stored
        diff_d diff_sum agreed agree_count flag
        f_marked f_start f_seeded f_preact f_state f_turned""".split()
        S = {n: sem(n) for n in names}
        block = ctx.enter_context(nc.Block())

        def bank(k):
            return ps[:, k, :]

        def half_scores(q, jh):
            return 2 + 2 * (q % 2) + jh

        def wait_y(eng, q):
            if q == 2:
                eng.wait_ge(S["y_ready_pool"], 1)
            else:
                eng.wait_ge(S["y_ready_dve"], {0: 2, 1: 3, 3: 4}[q])

        def ln_minus(eng, n):
            q, row, k = LN_PARTS[n]
            eng.tensor_tensor(y[:, q, row:row + k, :], xin[:, q, row:row + k, :],
                              stat[:, 0, q, row:row + k].unsqueeze(2).broadcast_to([P, k, C]),
                              ALU.subtract).then_inc(S["ln_centred"], 1)

        def ln_scale(eng, n, done):
            q, row, k = LN_PARTS[n]
            eng.tensor_tensor(y[:, q, row:row + k, :], y[:, q, row:row + k, :],
                              stat[:, 2, q, row:row + k].unsqueeze(2).broadcast_to([P, k, C]),
                              ALU.mult).then_inc(S[done], 1)

        ATT_BANK = [2, 3, 4, 5]
        WSUM_BANK = [6, 0, 6, 0]
        WX_BANK = [2, 3]

        def unit(t, k):
            return t[:, k // 2, 16 * (k % 2):16 * (k % 2 + 1), :]

        def wx_rows(k):
            return wx_q[:, 16 * (k % 2):16 * (k % 2 + 1), k // 2, :]

        def round_row(t):
            return (t - WARM) % SEG

        def side(t):
            return ((t - WARM) // SEG) % 2

        def state_out(t, r):
            if t >= WARM:
                return states[:, SEG * r + round_row(t), :, :]
            return warm[:, side(t), r, :, 1:C + 1]

        def state_in(t, r):
            if round_row(t) == 0:
                return start_state(side(t - 1), r)
            return state_out(t - 1, r)

        def start_state(k, r):
            if r == 0:
                return warm[:, k, STREAMS - 1, :, 0:C]
            return warm[:, k, r - 1, :, 1:C + 1]

        def order(t):
            moved = (t - WARM) // SEG - (-WARM) // SEG
            return [(moved + i) % STREAMS for i in range(STREAMS)]

        def count(t, r):
            return STREAMS * t + order(t).index(r) + 1

        STORED = 16 * len(STORES) * STREAMS
        FINAL_SIDE = side(WARM - 1)
        WARM_BANK = 0
        SEEDS = []
        for t in range(ROUNDS):
            if t == 0 or round_row(t) % ROWS == 0:
                SEEDS.append([t, 0])
            SEEDS[-1][1] += 1
        SEED_OF = [n for n, (t, k) in enumerate(SEEDS) for _ in range(k)]

        def rec_bank(t, r):
            return 2 * r + round_row(t) // ROWS

        def rec_slot(t, r):
            k = round_row(t) % ROWS
            return ps[:, rec_bank(t, r), P * k:P * (k + 1)]

        def seed_place(n, r):
            t, k = SEEDS[n]
            row, at = SEG * r + round_row(t), round_row(t) % ROWS
            return (bank(rec_bank(t, r))[:, P * at:P * (at + k)],
                    wx[:, row:row + k, :].rearrange("p i m -> p (i m)"))

        WARM_BANK = rec_bank(SEEDS[1][0], order(SEEDS[1][0])[-1])
        ACT_SEEDED = [(0, r) for r in order(0)[-1:]] + [(1, r) for r in order(SEEDS[1][0])[-1:]]
        DVE_SEEDED = [(n, r) for n in range(len(SEEDS)) for r in order(SEEDS[n][0]) if (n, r) not in ACT_SEEDED]

        def wait_seeded(eng, n, r):
            if (n, r) in ACT_SEEDED:
                eng.wait_ge(S["seeded_act"], ACT_SEEDED.index((n, r)) + 1)
            else:
                eng.wait_ge(S["seeded"], DVE_SEEDED.index((n, r)) + 1)

        def added_on_dve(n, r):
            return (n, order(WARM).index(r)) in ON_DVE

        ADDS = [(n, r) for n in range(len(PIECES)) for r in order(WARM)]

        def wait_added(eng, n, r):
            for own in (True, False):
                before = [k for k, a in enumerate([a for a in ADDS if added_on_dve(*a) == own]) if a[1] == r and a[0] <= n]
                if before:
                    eng.wait_ge(S["added_dve"] if own else S["added_pool"], before[-1] + 1)

        @block.sync
        def _(sp):
            def load_x(n):
                q, row, k = LN_PARTS[n]
                sp.dma_start(xin[:, q, row:row + k, :].rearrange("p i j -> p (i j)"),
                             x_dram[q][:, C * row:C * (row + k)]).then_inc(S[f"x_in{n}"], 16)

            def load_small(k, w, done):
                sp.dma_start(wsmall[:, k, :], bass.AP(w.tensor, 0, [[0, G], [C, C], [1, C]])).then_inc(S[done], 16)

            def load_gate(k, gate, done):
                sp.dma_start(gates[:, k:k + 1], bass.AP(gate.tensor, 0, [[0, P], [1, 1]])).then_inc(S[done], 16)

            def load_rel(dst, a, done):
                sp.dma_start(dst, a.rearrange("c h i -> c (h i)")).then_inc(S[done], 16)

            load_x(0)
            load_x(1)
            load_small(3, Wk, "wqk_in")
            load_small(4, Wq, "wqk_in")
            load_gate(0, Gq, "gates_in")
            load_gate(1, Gk, "gates_in")
            load_x(2)
            load_rel(r_in[0:C, :], rq, "r_in_s")
            load_rel(r_in[C:2 * C, :], rk, "r_in_s")
            load_x(3)
            load_x(4)
            load_rel(rv_in[:, :], rv, "rv_in")
            load_small(0, Wv, "w_in")
            load_small(1, W, "w_in")
            load_small(2, V, "w_in")
            load_gate(2, Gv1, "gates2_in")
            load_gate(3, Gv2, "gates2_in")
            for k, a in enumerate((gamma, beta)):
                sp.dma_start(affine[:, k:k + 1], bass.AP(a.tensor, 0, [[0, G], [1, C], [1, 1]])).then_inc(S["affine_in"], 16)
            for n, row, k in STORES:
                for r in order(WARM):
                    wait_added(sp, n, r)
                    rows = slice(SEG * r + row, SEG * r + row + k)
                    sp.dma_start(out_dram[:, :, C * rows.start:C * rows.stop],
                                 result[:, :, rows, :].rearrange("p q i j -> p q (i j)")).then_inc(S["stored"], 16)
            sp.wait_ge(S["flag"], 1)
            repeat = sp.value_load(repeat_flag[0:1, 0:1], min_val=0, max_val=1)
            with sp.If(repeat == 1):
                sp.wait_ge(S["f_turned"], 2 * BLOCKS)
                sp.dma_start(out_dram, result[:, :, :, :].rearrange("p q i j -> p q (i j)")).then_inc(S["stored"], 16)
                sp.wait_ge(S["stored"], STORED + 16)
            sp.wait_ge(S["stored"], STORED)

        def turn_back(row, k, r):
            rows = slice(SEG * r + row, SEG * r + row + k)
            at = P * (SEG * r + row)
            return nc.vector.transpose(back[:, at:at + P * k].rearrange("p (q i j) -> p i q j", q=Q, i=k),
                                       states[:, rows, :, :])

        def add_back(eng, row, k, r):
            rows = slice(SEG * r + row, SEG * r + row + k)
            at = P * (SEG * r + row)
            return eng.tensor_tensor(result[:, :, rows, :], back[:, at:at + P * k].rearrange("p (q i j) -> p q i j", q=Q, i=k),
                                     x2[:, :, rows, :], ALU.add)

        @block.gpsimd
        def _(pool):
            nc.gpsimd.memset(w_bd[:, :, :], 0.0)
            nc.gpsimd.memset(m_bd[:, :], 0.0)
            nc.gpsimd.memset(average[:, :, :], 0.0).then_inc(S["zeros"], 1)
            pool.wait_ge(S["zeros"], 1)
            for k in range(1 - G, G):
                ins = nc.gpsimd.affine_select(out=average[:, :, :], in_=average[:, :, :], compare_op=ALU.not_equal,
                                              fill=1.0 / G, base=C * k, pattern=[[-C, G], [-1, C]],
                                              channel_multiplier=1)
                ins.then_inc(S["average_set"], 1)
                pool.wait_ge(S["average_set"], k + G)
            nc.gpsimd.memset(r_tile[:, :], 0.0).then_inc(S["zeros"], 1)
            for n in range(2, len(LN_PARTS)):
                pool.wait_ge(S["ln_mean"], n + 1)
                ln_minus(nc.gpsimd, n)
            pool.wait_ge(S["ln_rstd"], POOL_SCALED + 1)
            pool.wait_ge(S["ln_squared"], POOL_SCALED + 1)
            ln_scale(nc.gpsimd, POOL_SCALED, "y_ready_pool")
            nc.gpsimd.memset(rv_bd[:, :, :], 0.0).then_inc(S["zeros"], 1)
            nc.gpsimd.memset(bn_eps[:, :], BN_EPS).then_inc(S["eps_set"], 1)
            nc.gpsimd.memset(ones[:, :], 1.0).then_inc(S["ones_set"], 1)
            nc.gpsimd.memset(warm[:, :, :, :, :], 0.0).then_inc(S["warm_zero"], 1)
            for q in range(Q):
                pool.wait_ge(S["score_max"], q + 1)
                nc.gpsimd.tensor_tensor(att[:, q, :, :], att[:, q, :, :],
                                        soft[:, 0, q, :].unsqueeze(2).broadcast_to([P, C, C]),
                                        ALU.subtract).then_inc(S["score_shifted"], 1)

            def centre(k):
                pool.wait_ge(S["t_mean"], k + 1)
                nc.gpsimd.tensor_tensor(unit(x2n, k), unit(x2, k), stat2[:, 0, k, :].unsqueeze(2).broadcast_to([P, C // 2, C]),
                                        ALU.subtract).then_inc(S["t_centred"], 1)

            def scale(k):
                pool.wait_ge(S["t_rstd"], k + 1)
                pool.wait_ge(S["t_squared"], k + 1)
                nc.gpsimd.tensor_tensor(unit(x2n, k), unit(x2n, k), stat2[:, 2, k, :].unsqueeze(2).broadcast_to([P, C // 2, C]),
                                        ALU.mult).then_inc(S["t_norm"], 1)

            centre(0)
            scale(0)
            centre(1)
            scale(1)
            centre(2)
            centre(3)
            scale(2)
            scale(3)
            centre(4)
            centre(5)
            scale(4)
            scale(5)
            centre(6)
            scale(6)
            for n, r in ADDS:
                if not added_on_dve(n, r):
                    pool.wait_ge(S["turned_back"], ADDS.index((n, r)) + 1)
                    add_back(nc.gpsimd, *PIECES[n], r).then_inc(S["added_pool"], 1)

        @block.scalar
        def _(act):
            def u_half(q, k):
                act.wait_ge(S["u_product"], 2 * q + k + 1)
                nc.scalar.copy(u_tile[:, IMG * q + BANK * k:IMG * q + BANK * (k + 1)], bank(k)).then_inc(S["u_half"], 1)

            def set_r(g):
                p = slice(C * g, C * (g + 1))
                act.wait_ge(S["r_product"], 1)
                act.wait_ge(S["zeros"], 2)
                nc.scalar.copy(r_bd[p, :, p], ps[p, 6:8, :].rearrange("p b (h i) -> p i (b h)", i=C)
                               ).then_inc(S["r_set"], 1)

            def set_rv():
                act.wait_ge(S["rv_product"], 1)
                act.wait_ge(S["zeros"], 3)
                for g in range(G):
                    p = slice(C * g, C * (g + 1))
                    nc.scalar.copy(rv_bd[p, :, p], ps[p, 6:8, :].rearrange("p b (i c) -> p (b i) c", c=C)
                                   ).then_inc(S["rv_set"], 1)

            def ln_square(n):
                q, row, k = LN_PARTS[n]
                act.wait_ge(S["ln_centred"], n + 1)
                if n >= 2:
                    act.wait_ge(S["ln_sum2"], n - 1)
                nc.scalar.activation(square[:, n % 2, 0:C * k], y[:, q, row:row + k, :].rearrange("p i j -> p (i j)"),
                                     ACT.Square).then_inc(S["ln_squared"], 1)

            for n, (q, row, k) in enumerate(LN_PARTS):
                if n != 4:
                    ln_square(n)
                if n == 1:
                    act.wait_ge(S["m_product"], 1)
                    act.wait_ge(S["zeros"], 1)
                    for g in range(G):
                        p = slice(C * g, C * (g + 1))
                        nc.scalar.mul(m_bd[p, p], ps[p, 6, 0:C], 1.0 / d).then_inc(S["m_set"], 1)
                if n >= 2:
                    set_r(n - 2)
                if n == 3:
                    ln_square(4)
                act.wait_ge(S["ln_var"], n + 1)
                nc.scalar.activation(stat[:, 2, q, row:row + k], stat[:, 1, q, row:row + k], ACT.Sqrt
                                     ).then_inc(S["ln_std"], 1)
                if n == 1:
                    u_half(0, 0)
                    u_half(0, 1)
            set_r(3)
            u_half(1, 0)
            u_half(1, 1)
            u_half(2, 0)
            u_half(2, 1)
            for b in range(BLOCKS):
                act.wait_ge(S["rel_product"], b + 1)
                nc.scalar.copy(rel[:, :, ROWS * b:ROWS * (b + 1), :],
                               bank(6 + b % 2).rearrange("p (i q j) -> p q i j", i=ROWS, q=Q)).then_inc(S["rel_ready"], 1)
            def value_out(k):
                act.wait_ge(S["value_product"], k + 1)
                nc.scalar.copy(unit(values, k), bank(k % 2).rearrange("p (h j) -> p h j", j=C)
                               ).then_inc(S["value_half"], 1)

            for q in range(Q):
                act.wait_ge(S["score_shifted"], q + 1)
                nc.scalar.activation(att[:, q, :, :].rearrange("p i j -> p (i j)"),
                                     att[:, q, :, :].rearrange("p i j -> p (i j)"), ACT.Exp).then_inc(S["score_exp"], 1)
                if q == 0:
                    u_half(Q - 1, 0)
                    u_half(Q - 1, 1)
                if q == 1:
                    value_out(0)
                    value_out(1)
                    set_rv()
                    value_out(2)
                if q == 2:
                    value_out(3)
                    value_out(4)
            for k in (5, 6, 7):
                value_out(k)

            def t_square(k):
                if k < UNITS - 1:
                    act.wait_ge(S["t_centred"], k + 1)
                else:
                    act.wait_ge(S["t_centred_dve"], 1)
                if k >= 2:
                    act.wait_ge(S["t_sum2"], k - 1)
                nc.scalar.activation(square[:, k % 2, 0:BANK].rearrange("p (i j) -> p i j", j=C),
                                     unit(x2n, k), ACT.Square).then_inc(S["t_squared"], 1)

            def t_std(k):
                act.wait_ge(S["t_var"], k + 1)
                nc.scalar.activation(stat2[:, 2, k, :], stat2[:, 1, k, :], ACT.Sqrt).then_inc(S["t_std"], 1)

            def wx_out(k):
                act.wait_ge(S["wx_product"], k + 1)
                nc.scalar.copy(wx_rows(k), bank(WX_BANK[k % 2]).rearrange("p (i c) -> p i c", c=C)).then_inc(S["wx_ready"], 1)

            t_square(0)
            t_std(0)
            t_square(1)
            t_std(1)
            t_square(2)
            t_std(2)
            t_square(3)
            wx_out(0)
            t_std(3)
            t_square(4)
            wx_out(1)
            wx_out(2)
            t_square(5)
            t_std(4)
            wx_out(3)
            t_std(5)
            t_square(6)
            t_square(7)
            t_std(6)
            t_std(7)
            wx_out(4)
            wx_out(5)
            wx_out(6)
            wx_out(7)
            act.wait_ge(S["bn_var"], 1)
            act.wait_ge(S["eps_set"], 1)
            nc.scalar.activation(std, ps[:, 7, 1:2], ACT.Sqrt, bias=bn_eps[:, :]).then_inc(S["bn_std"], 1)
            nc.scalar.activation(table_load[:, :], bn_eps[:, :], ACT.Sigmoid)
            act.wait_ge(S["bn_shift"], 1)

            def act_seeds(n):
                for m, r in ACT_SEEDED:
                    if m == n:
                        if rec_bank(SEEDS[n][0], r) == WARM_BANK:
                            act.wait_ge(S["warmed"], 1)
                        out, rows = seed_place(n, r)
                        nc.scalar.activation(out, rows, ACT.Identity, bias=shift, scale=scl
                                             ).then_inc(S["seeded_act"], 1)

            act_seeds(0)

            for t in range(ROUNDS):
                for r in order(t):
                    if t == 0:
                        wait_seeded(act, 0, r)
                        act.wait_ge(S["warm_zero"], 1)
                    else:
                        act.wait_ge(S["preact"], count(t, r) - STREAMS)
                    nc.scalar.activation(state_out(t, r), rec_slot(t, r).rearrange("p (q c) -> p q c", q=Q),
                                         ACT.Sigmoid).then_inc(S["state"], 1)
                if t == 0:
                    act_seeds(1)

            act.wait_ge(S["flag"], 1)
            repeat = act.value_load(repeat_flag[0:1, 0:1], min_val=0, max_val=1)
            with act.If(repeat == 1):
                with act.Fori(0, SEGMENTS - 1) as n:
                    for s in range(SEG):
                        for r in range(STREAMS):
                            act.wait_ge(S["f_preact"], n * (SEG * STREAMS) + (STREAMS * s + r + 1))
                            nc.scalar.activation(states[:, SEG * r + s, :, :],
                                                 rec_slot(WARM + s, r).rearrange("p (q c) -> p q c", q=Q),
                                                 ACT.Sigmoid).then_inc(S["f_state"], 1)

        @block.vector
        def _(dve):
            def spread_out(dst, src, gate, factor):
                nc.vector.tensor_scalar(dst.rearrange("p (g c) -> p g c", g=G),
                                        src.unsqueeze(1).broadcast_to([C, G, C]), gate, factor,
                                        ALU.mult, ALU.mult).then_inc(S["w_spread"], 1)

            def setup_weights():
                dve.wait_ge(S["wqk_in"], 32)
                dve.wait_ge(S["gates_in"], 32)
                spread_out(spread[0:C, :], wsmall[0:C, 4, :], gates[0:C, 0:1], 1.0 / d)
                spread_out(spread[C:2 * C, :], wsmall[C:2 * C, 3, :], gates[C:2 * C, 1:2], 1.0 / d)

            def setup_turned():
                dve.wait_ge(S["gates2_in"], 32)
                dve.wait_ge(S["average_set"], 2 * G - 1)
                spread_out(spread_v[:, :], average[0:C, 0, :], gates[0:C, 3:4], float(G))
                dve.wait_ge(S["w_in"], 16 * 3)
                nc.vector.transpose(wturned[:, :, :], wsmall[:, 0:3, :]).then_inc(S["turned"], 1)
                dve.wait_ge(S["turned"], 1)
                dve.wait_ge(S["zeros"], 1)
                for g in range(G):
                    p = slice(C * g, C * (g + 1))
                    nc.vector.tensor_scalar(w_bd[p, 0, p], wturned[p, 0, :], gates[p, 2:3], None,
                                            ALU.mult).then_inc(S["w_set"], 1)
                    nc.vector.tensor_copy(w_bd[p, 1:3, p], wturned[p, 1:3, :]).then_inc(S["w_set"], 1)
                dve.wait_ge(S["rv_in"], 16)
                nc.vector.transpose(rv_t[:, :, :], rv_in[:, :].rearrange("p (h i) -> p i h", h=C)
                                    ).then_inc(S["rv_turned"], 1)

            def ln_mean(n):
                q, row, k = LN_PARTS[n]
                rows = slice(row, row + k)
                dve.wait_ge(S[f"x_in{n}"], 16)
                nc.vector.tensor_reduce(stat[:, 1, q, rows], xin[:, q, rows, :], AX_X, ALU.add).then_inc(S["ln_sum"], 1)
                dve.wait_ge(S["ln_sum"], n + 1)
                nc.vector.tensor_scalar(stat[:, 0, q, rows], stat[:, 1, q, rows], 1.0 / C, None,
                                        ALU.mult).then_inc(S["ln_mean"], 1)

            def ln_var(n):
                q, row, k = LN_PARTS[n]
                rows = slice(row, row + k)
                dve.wait_ge(S["ln_squared"], n + 1)
                nc.vector.tensor_reduce(stat[:, 0, q, rows], square[:, n % 2, 0:C * k].rearrange("p (i j) -> p i j", j=C),
                                        AX_X, ALU.add).then_inc(S["ln_sum2"], 1)
                dve.wait_ge(S["ln_sum2"], n + 1)
                nc.vector.tensor_scalar(stat[:, 1, q, rows], stat[:, 0, q, rows], 1.0 / C, LN1_EPS,
                                        ALU.mult, ALU.add).then_inc(S["ln_var"], 1)

            def ln_rstd(n):
                q, row, k = LN_PARTS[n]
                dve.wait_ge(S["ln_std"], n + 1)
                nc.vector.reciprocal(stat[:, 2, q, row:row + k], stat[:, 2, q, row:row + k]).then_inc(S["ln_rstd"], 1)

            for n in range(2):
                ln_mean(n)
                dve.wait_ge(S["ln_mean"], n + 1)
                ln_minus(nc.vector, n)
            for n in range(2):
                ln_var(n)
                ln_rstd(n)
                dve.wait_ge(S["ln_rstd"], n + 1)
                ln_scale(nc.vector, n, "y_ready_dve")
            setup_weights()
            for n in range(2, len(LN_PARTS)):
                ln_mean(n)
            for n in range(2, len(LN_PARTS)):
                ln_var(n)
                ln_rstd(n)
                if n != POOL_SCALED:
                    dve.wait_ge(S["ln_rstd"], n + 1)
                    ln_scale(nc.vector, n, "y_ready_dve")
            setup_turned()
            def turn_values(q):
                dve.wait_ge(S["value_half"], 2 * q + 2)
                nc.vector.transpose(v_t[:, q, :, :], values[:, q, :, :].rearrange("p h j -> p j h")
                                    ).then_inc(S["v_turned"], 1)

            def score_max(q):
                dve.wait_ge(S["score_product"], 2 * q + 2)
                dve.wait_ge(S["rel_ready"], BLOCKS)
                nc.vector.tensor_tensor(att[:, q, :, :],
                                        ps[:, half_scores(q, 0):half_scores(q, 0) + 2, :]
                                        .rearrange("p b (j i) -> p i (b j)", i=C),
                                        rel[:, q, :, :], ALU.add).then_inc(S["score_sum"], 1)
                dve.wait_ge(S["score_sum"], q + 1)
                nc.vector.tensor_reduce(soft[:, 0, q, :], att[:, q, :, :], AX_X, ALU.max).then_inc(S["score_max"], 1)

            def weights(q):
                dve.wait_ge(S["score_exp"], q + 1)
                nc.vector.tensor_reduce(soft[:, 1, q, :], att[:, q, :, :], AX_X, ALU.add).then_inc(S["weight_sum"], 1)
                dve.wait_ge(S["weight_sum"], q + 1)
                nc.vector.reciprocal(soft[:, 1, q, :], soft[:, 1, q, :]).then_inc(S["weight_recip"], 1)
                dve.wait_ge(S["weight_recip"], q + 1)
                nc.vector.tensor_tensor(att[:, q, :, :], att[:, q, :, :],
                                        soft[:, 1, q, :].unsqueeze(2).broadcast_to([P, C, C]),
                                        ALU.mult).then_inc(S["weights"], 1)

            for t in range(Q + 1):
                if t < Q:
                    score_max(t)
                if t >= 2:
                    turn_values(t - 2)
                if t >= 1:
                    weights(t - 1)
            turn_values(Q - 1)

            def add_relative(b):
                rows = slice(ROWS * b, ROWS * (b + 1))
                dve.wait_ge(S["relv_product"], b + 1)
                nc.vector.tensor_tensor(x2[:, :, rows, :],
                                        bank(ATT_BANK[b % 4]).rearrange("p (q i j) -> p q i j", q=Q, i=ROWS),
                                        xin[:, :, rows, :], ALU.add).then_inc(S["x2_part"], 1)

            def residual(k):
                dve.wait_ge(S["x2_part"], 4 * (k % 2 + 1))
                dve.wait_ge(S["wsum_product"], 2 * (k // 2) + 2)
                first = WSUM_BANK[k // 2]
                nc.vector.tensor_tensor(unit(x2, k),
                                        ps[:, first:first + 2, :].rearrange("p b (j i) -> p i (b j)", i=C)
                                        [:, 16 * (k % 2):16 * (k % 2 + 1), :],
                                        unit(x2, k), ALU.add).then_inc(S["x2_ready"], 1)
                dve.wait_ge(S["x2_ready"], k + 1)
                nc.vector.tensor_reduce(stat2[:, 1, k, :], unit(x2, k), AX_X, ALU.add).then_inc(S["t_sum"], 1)
                dve.wait_ge(S["t_sum"], k + 1)
                nc.vector.tensor_scalar(stat2[:, 0, k, :], stat2[:, 1, k, :], 1.0 / C, None, ALU.mult).then_inc(S["t_mean"], 1)
                if k == UNITS - 1:
                    dve.wait_ge(S["t_mean"], k + 1)
                    nc.vector.tensor_tensor(unit(x2n, k), unit(x2, k),
                                            stat2[:, 0, k, :].unsqueeze(2).broadcast_to([P, C // 2, C]),
                                            ALU.subtract).then_inc(S["t_centred_dve"], 1)

            def t_var(k):
                dve.wait_ge(S["t_squared"], k + 1)
                nc.vector.tensor_reduce(stat2[:, 0, k, :], square[:, k % 2, 0:BANK].rearrange("p (m j) -> p m j", j=C),
                                        AX_X, ALU.add).then_inc(S["t_sum2"], 1)
                dve.wait_ge(S["t_sum2"], k + 1)
                nc.vector.tensor_scalar(stat2[:, 1, k, :], stat2[:, 0, k, :], 1.0 / C, LN2_EPS,
                                        ALU.mult, ALU.add).then_inc(S["t_var"], 1)

            def t_rstd(k):
                dve.wait_ge(S["t_std"], k + 1)
                nc.vector.reciprocal(stat2[:, 2, k, :], stat2[:, 2, k, :]).then_inc(S["t_rstd"], 1)
                if k == UNITS - 1:
                    dve.wait_ge(S["t_rstd"], k + 1)
                    dve.wait_ge(S["t_squared"], k + 1)
                    nc.vector.tensor_tensor(unit(x2n, k), unit(x2n, k),
                                            stat2[:, 2, k, :].unsqueeze(2).broadcast_to([P, C // 2, C]),
                                            ALU.mult).then_inc(S["t_norm_dve"], 1)

            def t_turn(k):
                if k < UNITS - 1:
                    dve.wait_ge(S["t_norm"], k + 1)
                else:
                    dve.wait_ge(S["t_norm_dve"], 1)
                nc.vector.transpose(tokens[:, 16 * (k % 2):16 * (k % 2 + 1), k // 2, :], unit(x2n, k)
                                    ).then_inc(S["t_turned"], 1)

            def bn_part(k):
                dve.wait_ge(S["wx_ready"], k + 1)
                nc.vector.bn_stats(bn[:, k, :], wx_rows(k)).then_inc(S["bn_part"], 1)

            add_relative(0)
            add_relative(1)
            add_relative(2)
            add_relative(3)
            residual(0)
            add_relative(4)
            add_relative(5)
            t_var(0)
            add_relative(6)
            t_rstd(0)
            add_relative(7)
            residual(1)
            residual(2)
            t_turn(0)
            t_var(1)
            t_rstd(1)
            residual(3)
            t_turn(1)
            t_var(2)
            t_rstd(2)
            t_var(3)
            t_rstd(3)
            bn_part(0)
            residual(4)
            t_turn(2)
            t_turn(3)
            residual(5)
            bn_part(1)
            t_var(4)
            bn_part(2)
            t_rstd(4)
            t_var(5)
            t_rstd(5)
            t_turn(4)
            bn_part(3)
            residual(6)
            residual(7)
            t_var(6)
            t_rstd(6)
            t_var(7)
            t_turn(5)
            t_turn(6)
            t_rstd(7)
            t_turn(7)
            bn_part(4)
            dve.wait_ge(S["marked"], 2)
            nc.vector.memset(ps[:, 7, 0:2], 0.0).then_inc(S["bn_zero"], 1)
            bn_part(5)
            bn_part(6)
            bn_part(7)
            gmean, gvar, off, spr, negmean = (bnv[:, k:k + 1] for k in range(5))
            dve.wait_ge(S["bn_part"], BLOCKS)
            nc.vector.bn_aggr(bnv[:, 0:2], bn[:, :, :]).then_inc(S["bn_group"], 1)
            dve.wait_ge(S["bn_mean"], 1)
            nc.vector.tensor_tensor(off, gmean, ps[:, 7, 0:1], ALU.subtract).then_inc(S["bn_off"], 1)
            nc.vector.tensor_scalar(negmean, ps[:, 7, 0:1], -1.0, None, ALU.mult).then_inc(S["bn_mean_s"], 1)
            dve.wait_ge(S["bn_off"], 1)
            nc.vector.scalar_tensor_tensor(out=spr, in0=off, scalar=off, in1=gvar, op0=ALU.mult,
                                           op1=ALU.add).then_inc(S["bn_spread"], 1)
            dve.wait_ge(S["bn_std"], 1)
            dve.wait_ge(S["affine_in"], 32)
            nc.vector.reciprocal(std, std).then_inc(S["bn_rstd"], 1)
            dve.wait_ge(S["bn_rstd"], 1)
            nc.vector.tensor_tensor(scl, std, affine[:, 0:1], ALU.mult).then_inc(S["bn_scale"], 1)
            dve.wait_ge(S["bn_scale"], 1)
            dve.wait_ge(S["bn_mean_s"], 1)
            nc.vector.scalar_tensor_tensor(out=shift, in0=scl, scalar=negmean, in1=affine[:, 1:2], op0=ALU.mult,
                                           op1=ALU.add).then_inc(S["bn_shift"], 1)
            dve.wait_ge(S["bn_shift"], 1)

            def seed(n, r):
                out, rows = seed_place(n, r)
                return nc.vector.tensor_scalar(out, rows, scl, shift, ALU.mult, ALU.add)

            def seeds(n):
                for r in [r for m, r in DVE_SEEDED if m == n]:
                    if n == 1 and rec_bank(SEEDS[1][0], r) == WARM_BANK:
                        dve.wait_ge(S["warmed"], 1)
                    if n >= 2:
                        dve.wait_ge(S["state"], count(SEEDS[n - 1][0] - 1, r))
                    seed(n, r).then_inc(S["seeded"], 1)

            def finish(n):
                row, k = PIECES[n]
                for r in order(WARM):
                    dve.wait_ge(S["state"], count(WARM + row + k - 1, r))
                    turn_back(row, k, r).then_inc(S["turned_back"], 1)
                for r in order(WARM):
                    if added_on_dve(n, r):
                        dve.wait_ge(S["turned_back"], ADDS.index((n, r)) + 1)
                        add_back(nc.vector, row, k, r).then_inc(S["added_dve"], 1)

            for n in range(len(SEEDS)):
                seeds(n)
            for n in range(len(PIECES)):
                finish(n)

            dve.wait_ge(S["state"], STREAMS * ROUNDS)
            nc.vector.tensor_tensor(diff[:, 0, :].rearrange("p (r q c) -> p r q c", r=STREAMS, q=Q),
                                    states[:, SEG - 1::SEG, :, :], warm[:, FINAL_SIDE, :, :, 1:C + 1],
                                    ALU.subtract).then_inc(S["diff_d"], 1)
            dve.wait_ge(S["diff_d"], 1)
            nc.vector.tensor_tensor_reduce(diff[:, 1, :], diff[:, 0, :], diff[:, 0, :], 1.0, 0.0,
                                           ALU.mult, ALU.add, diffsum[:, :]).then_inc(S["diff_sum"], 1)
            dve.wait_ge(S["diff_sum"], 1)
            nc.vector.tensor_scalar(agreed[:, :], diffsum[:, :], AGREE * AGREE, None, ALU.is_le).then_inc(S["agreed"], 1)
            dve.wait_ge(S["agree_count"], 1)
            nc.vector.tensor_scalar(repeat_flag[:, :], ps[0:1, 0, 0:1], float(P), None,
                                    ALU.is_lt).then_inc(S["flag"], 1)
            dve.wait_ge(S["flag"], 1)
            repeat = dve.value_load(repeat_flag[0:1, 0:1], min_val=0, max_val=1)
            with dve.If(repeat == 1):
                PASS = SEG * STREAMS
                dve.wait_ge(S["f_marked"], 1)
                with dve.Fori(0, SEGMENTS - 1) as n:
                    nc.vector.tensor_copy(warm[:, FINAL_SIDE, :, :, 1:C + 1], states[:, SEG - 1::SEG, :, :]).then_inc(S["f_start"], 1)
                    for h in range(GROUPS):
                        for r in range(STREAMS):
                            seed(len(SEEDS) - GROUPS + h, r).then_inc(S["f_seeded"], 1)
                    dve.wait_ge(S["f_state"], n * PASS + PASS)
                dve.wait_ge(S["stored"], STORED)
                for h in range(GROUPS):
                    for r in range(STREAMS):
                        n = GROUPS * (STREAMS * h + r)
                        turn_back(ROWS * h, ROWS, r).then_inc(S["f_turned"], 1)
                        dve.wait_ge(S["f_turned"], n + 1)
                        add_back(nc.vector, ROWS * h, ROWS, r).then_inc(S["f_turned"], 1)
                        dve.wait_ge(S["f_turned"], n + 2)

        @block.tensor
        def _(pe):
            pe.wait_ge(S["wqk_in"], 32)
            for g in range(G):
                p = slice(C * g, C * (g + 1))
                ins = nc.tensor.matmul(ps[p, 6, 0:C], wsmall[p, 3, :], wsmall[p, 4, :], start=True, stop=True)
            ins.then_inc(S["m_product"], 1)

            def keep_warm(k, n):
                for _ in range(n):
                    ins = nc.tensor.matmul(bank(k), xin[:, 0, 0:4, :].rearrange("p i j -> p (i j)"),
                                           xin[:, 0, 0:16, :].rearrange("p i j -> p (i j)"),
                                           start=True, stop=True)
                return ins

            pe.wait_ge(S["x_in0"], 16)
            keep_warm(2, 3)
            pe.wait_ge(S["m_set"], G)

            def project_u(q):
                wait_y(pe, q)
                for k in range(2):
                    if q >= 1:
                        pe.wait_ge(S["u_half"], 2 * (q - 1) + k + 1)
                    nc.tensor.matmul(bank(k), m_bd[:, :], y[:, q, 16 * k:16 * (k + 1), :].rearrange("p i j -> p (i j)"),
                                     start=True, stop=True).then_inc(S["u_product"], 1)

            def scores(q, jh):
                pe.wait_ge(S["u_half"], 2 * q + 2)
                if q >= 2:
                    pe.wait_ge(S["score_sum"], q - 1)
                for j in range(16 * jh, 16 * (jh + 1)):
                    for g in range(G):
                        p = slice(C * g, C * (g + 1))
                        ins = nc.tensor.matmul(ps[p, half_scores(q, j // 16), C * (j % 16):C * (j % 16 + 1)],
                                               u[p, q, :, j], y[p, q, :, j], start=True, stop=True)
                ins.then_inc(S["score_product"], 1)

            def relative_factor():
                pe.wait_ge(S["w_spread"], 2)
                pe.wait_ge(S["r_in_s"], 16 * 2)
                for k in range(2):
                    cols = slice(BANK * k, BANK * (k + 1))
                    ins = nc.tensor.matmul(bank(6 + k), spread[:, :], r_in[:, cols], start=True, stop=True)
                ins.then_inc(S["r_product"], 1)

            def relative_values():
                pe.wait_ge(S["rel_ready"], BLOCKS)
                pe.wait_ge(S["w_spread"], 3)
                pe.wait_ge(S["rv_turned"], 1)
                for k in range(2):
                    ins = nc.tensor.matmul(bank(6 + k), spread_v[:, :],
                                           rv_t[:, 16 * k:16 * (k + 1), :].rearrange("p i c -> p (i c)"),
                                           start=True, stop=True)
                ins.then_inc(S["rv_product"], 1)

            def project_values(k):
                pe.wait_ge(S["w_set"], 2 * G)
                if k < 2:
                    pe.wait_ge(S["u_half"], 2 * Q)
                else:
                    pe.wait_ge(S["value_half"], k - 1)
                nc.tensor.matmul(bank(k % 2), w_bd[:, 0, :], unit(y, k).rearrange("p i j -> p (i j)"),
                                 start=True, stop=True).then_inc(S["value_product"], 1)

            def relative_scores():
                pe.wait_ge(S["r_set"], G)
                for b in range(BLOCKS):
                    if b >= 2:
                        pe.wait_ge(S["rel_ready"], b - 1)
                    for k in range(ROWS):
                        ins = nc.tensor.matmul(bank(6 + b % 2)[:, P * k:P * (k + 1)], r_bd[:, ROWS * b + k, :],
                                               y[:, :, ROWS * b + k, :], start=True, stop=True)
                    ins.then_inc(S["rel_product"], 1)

            project_u(0)
            relative_factor()
            scores(0, 0)
            scores(0, 1)
            project_u(1)
            project_u(2)
            wait_y(pe, Q - 1)
            relative_scores()

            def weighted_sums(q, jh):
                pe.wait_ge(S["weights"], q + 1)
                pe.wait_ge(S["v_turned"], q + 1)
                if q == 0:
                    pe.wait_ge(S["rv_set"], G)
                elif q == 1:
                    pe.wait_ge(S["value_half"], UNITS)
                else:
                    pe.wait_ge(S["x2_ready"], 2 * (q - 1))
                for j in range(16 * jh, 16 * (jh + 1)):
                    for g in range(G):
                        p = slice(C * g, C * (g + 1))
                        ins = nc.tensor.matmul(ps[p, WSUM_BANK[q] + jh, C * (j % 16):C * (j % 16 + 1)],
                                               v_t[p, q, j, :], att[p, q, :, j], start=True, stop=True)
                ins.then_inc(S["wsum_product"], 1)

            def value_rows(b):
                if b < 4:
                    pe.wait_ge(S["weights"], Q)
                    pe.wait_ge(S["rv_set"], G)
                else:
                    pe.wait_ge(S["x2_part"], b - 3)
                rows = bank(ATT_BANK[b % 4]).rearrange("p (q i j) -> p q i j", q=Q, i=ROWS)
                for k in range(ROWS):
                    ins = nc.tensor.matmul(rows[:, :, k, :], rv_bd[:, ROWS * b + k, :], att[:, :, ROWS * b + k, :],
                                           start=(k == 0), stop=True, skip_group_check=True)
                ins.then_inc(S["relv_product"], 1)

            def mark_bank(k):
                pe.wait_ge(S["x2_ready"], UNITS - 2 if k >= 6 else UNITS)
                keep_warm(k, 1).then_inc(S["marked"], 1)

            def project_wx(k):
                pe.wait_ge(S["t_turned"], k + 1)
                if k < 2:
                    pe.wait_ge(S["x2_part"], 5 + k)
                else:
                    pe.wait_ge(S["wx_ready"], k - 1)
                nc.tensor.matmul(bank(WX_BANK[k % 2]), w_bd[:, 1, :],
                                 tokens[:, 16 * (k % 2):16 * (k % 2 + 1), k // 2, :],
                                 start=True, stop=True).then_inc(S["wx_product"], 1)

            scores(1, 0)
            scores(1, 1)
            project_u(3)
            scores(2, 0)
            project_values(0)
            project_values(1)
            scores(2, 1)
            project_values(2)
            project_values(3)
            relative_values()
            scores(3, 0)
            scores(3, 1)
            weighted_sums(0, 0)
            project_values(4)
            project_values(5)
            project_values(6)
            weighted_sums(0, 1)
            project_values(7)
            value_rows(0)
            value_rows(1)
            value_rows(2)
            weighted_sums(1, 0)
            value_rows(3)
            value_rows(4)
            value_rows(5)
            weighted_sums(1, 1)
            value_rows(6)
            value_rows(7)
            weighted_sums(2, 0)
            weighted_sums(2, 1)
            project_wx(0)
            pe.wait_ge(S["x2_part"], BLOCKS)
            keep_warm(4, 1)
            weighted_sums(3, 0)
            project_wx(1)
            project_wx(2)
            project_wx(3)
            weighted_sums(3, 1)
            project_wx(4)
            mark_bank(6)
            mark_bank(7)
            mark_bank(0)
            pe.wait_ge(S["x2_part"], BLOCKS)
            keep_warm(4, 1)
            mark_bank(1)
            project_wx(5)
            project_wx(6)
            project_wx(7)
            pe.wait_ge(S["bn_zero"], 1)
            pe.wait_ge(S["bn_group"], 1)
            avg = average[:, :, :].rearrange("p g c -> p (g c)")
            nc.tensor.matmul(ps[:, 7, 0:1], avg, bnv[:, 0:1], start=False, stop=True,
                             skip_group_check=True).then_inc(S["bn_mean"], 1)
            pe.wait_ge(S["bn_spread"], 1)
            nc.tensor.matmul(ps[:, 7, 1:2], avg, bnv[:, 3:4], start=False, stop=True,
                             skip_group_check=True).then_inc(S["bn_var"], 1)

            keep_warm(WARM_BANK, 2).then_inc(S["warmed"], 1)

            for t in range(1, ROUNDS):
                for r in order(t):
                    if t == 1 or SEED_OF[t] > SEED_OF[t - 1]:
                        wait_seeded(pe, SEED_OF[t], r)
                    source = (r - 1) % STREAMS if round_row(t) == 0 else r
                    pe.wait_ge(S["state"], count(t - 1, source))
                    nc.tensor.matmul(rec_slot(t, r), w_bd[:, 2, :], state_in(t, r), start=False, stop=True,
                                     skip_group_check=True).then_inc(S["preact"], 1)

            pe.wait_ge(S["agreed"], 1)
            nc.tensor.matmul(ps[0:1, 0, 0:1], agreed[:, :], ones[:, :], start=True, stop=True).then_inc(S["agree_count"], 1)
            pe.wait_ge(S["flag"], 1)
            repeat = pe.value_load(repeat_flag[0:1, 0:1], min_val=0, max_val=1)
            with pe.If(repeat == 1):
                nc.tensor.matmul(bank(0), w_bd[:, 2, :], wx[:, 0:ROWS, :].rearrange("p i m -> p (i m)"),
                                 start=True, stop=True).then_inc(S["f_marked"], 1)
                with pe.Fori(0, SEGMENTS - 1) as n:
                    pe.wait_ge(S["f_start"], n + 1)
                    for s in range(SEG):
                        for r in range(STREAMS):
                            if s % ROWS == 0:
                                pe.wait_ge(S["f_seeded"], n * (GROUPS * STREAMS) + (STREAMS * (s // ROWS) + r + 1))
                            if s > 0:
                                pe.wait_ge(S["f_state"], n * (SEG * STREAMS) + (STREAMS * (s - 1) + r + 1))
                            nc.tensor.matmul(rec_slot(WARM + s, r), w_bd[:, 2, :],
                                             start_state(FINAL_SIDE, r) if s == 0 else states[:, SEG * r + s - 1, :, :],
                                             start=False, stop=True, skip_group_check=True).then_inc(S["f_preact"], 1)


_INS = ["x", "L0_conv_Wq", "L0_conv_Wk", "L0_conv_Wv", "L0_conv_rq", "L0_conv_rk", "L0_conv_rv", "L0_conv_Gq",
        "L0_conv_Gk", "L0_conv_Gv1", "L0_conv_Gv2", "L0_ffn_W", "L0_ffn_V", "L0_ffn_gamma", "L0_ffn_beta"]
_OUTS = [((16, 32, 32, 32), "float32")]


def kernel(**inputs):
    import numpy as _np
    import concourse.bacc as _bacc
    from concourse import mybir as _mybir
    from concourse.bass_utils import run_bass_kernel_spmd as _run

    nc = _bacc.Bacc("TRN2", target_bir_lowering=False, num_devices=1)
    arrays, args = {}, []
    for name in _INS:
        a = _np.ascontiguousarray(inputs[name])
        arrays[f"in_{name}_dram"] = a
        args.append(nc.dram_tensor(f"in_{name}_dram", a.shape, _mybir.dt.from_np(a.dtype), kind="ExternalInput").ap())
    for i, (shape, dtype) in enumerate(_OUTS):
        dt = _mybir.dt.from_np(_np.dtype(dtype))
        args.append(nc.dram_tensor(f"out_{i}_dram", shape, dt, kind="ExternalOutput").ap())
    metaformer_kernel(nc, *args)
    r = _run(nc, [arrays], core_ids=[0])
    got = tuple(r.results[0][f"out_{i}_dram"] for i in range(len(_OUTS)))
    return got[0]
```
